# Optimizing a Trainium2 kernel written in Bass

```python
import numpy as np
import jax
import jax.numpy as jnp

def _softmax(x, axis=-1):
    return jax.nn.softmax(x, axis=axis)

def _gelu(x):
    return jax.nn.gelu(x, approximate=True)

def _silu(x):
    return jax.nn.silu(x)

def _sigmoid(x):
    return jax.nn.sigmoid(x)

def _layernorm(x, axis=-1, eps=1e-05):
    m = jnp.mean(x, axis=axis, keepdims=True)
    v = jnp.var(x, axis=axis, keepdims=True)
    return (x - m) / jnp.sqrt(v + eps)

def _scatter_add(tgt, idx, src, axis=0):
    return tgt.at[idx].add(src)

def _segment_sum(src, seg, n):
    return jax.ops.segment_sum(src, seg, n)
kernel_name = 'mk_prb_d1_jaxref_r8_ce2649'

def setup_inputs(seed: int=0):
    np.random.seed(seed)
    _w = jnp.asarray

    def _L0_attn_setup():
        import jax, jax.numpy as jnp
        import numpy as np
        N_HEADS = 16
        D_HEAD = 128
        D_MODEL = 256
        MAXLEN = 256
        key = jax.random.key(seed)
        ks = jax.random.split(key, 9)
        b, t = (2, 256)
        hd = N_HEADS * D_HEAD
        init = 0.02
        return {'x': jax.random.normal(ks[0], (b, t, D_MODEL), dtype=jnp.float32), 'Wq': jax.random.normal(ks[1], (D_MODEL, hd), dtype=jnp.float32) * init, 'bq': jnp.zeros((hd,), dtype=jnp.float32), 'Wk': jax.random.normal(ks[2], (D_MODEL, hd), dtype=jnp.float32) * init, 'bk': jnp.zeros((hd,), dtype=jnp.float32), 'Wv': jax.random.normal(ks[3], (D_MODEL, hd), dtype=jnp.float32) * init, 'bv': jnp.zeros((hd,), dtype=jnp.float32), 'Wo': jax.random.normal(ks[4], (hd, D_MODEL), dtype=jnp.float32) * init, 'bo': jnp.zeros((D_MODEL,), dtype=jnp.float32)}
    _L0_attn_in = _L0_attn_setup()

    def _L0_ffn_setup():
        import jax, jax.numpy as jnp
        import numpy as np
        DIM_IN = 256
        DIM_HIDDEN = 1024
        key = jax.random.key(seed)
        k_x, k_g, k_u, k_d = jax.random.split(key, 4)
        s_in = 1.0 / np.sqrt(DIM_IN)
        s_hid = 1.0 / np.sqrt(DIM_HIDDEN)
        x = jax.random.normal(k_x, (4, 256, DIM_IN), dtype=jnp.float32)
        w_gate = jax.random.uniform(k_g, (DIM_HIDDEN, DIM_IN), jnp.float32, -s_in, s_in)
        w_up = jax.random.uniform(k_u, (DIM_HIDDEN, DIM_IN), jnp.float32, -s_in, s_in)
        w_down = jax.random.uniform(k_d, (DIM_IN, DIM_HIDDEN), jnp.float32, -s_hid, s_hid)
        return {'x': x, 'w_gate': w_gate, 'w_up': w_up, 'w_down': w_down}
    _L0_ffn_in = _L0_ffn_setup()
    _d = {'L0_attn_x': _L0_attn_in['x'], 'L0_attn_Wq': _L0_attn_in['Wq'], 'L0_attn_bq': _L0_attn_in['bq'], 'L0_attn_Wk': _L0_attn_in['Wk'], 'L0_attn_bk': _L0_attn_in['bk'], 'L0_attn_Wv': _L0_attn_in['Wv'], 'L0_attn_bv': _L0_attn_in['bv'], 'L0_attn_Wo': _L0_attn_in['Wo'], 'L0_attn_bo': _L0_attn_in['bo'], 'L0_ffn_w_gate': _L0_ffn_in['w_gate'], 'L0_ffn_w_up': _L0_ffn_in['w_up'], 'L0_ffn_w_down': _L0_ffn_in['w_down']}
    _x0 = _d['L0_attn_x']
    _d['L0_attn_x'] = jax.random.normal(jax.random.fold_in(jax.random.key(seed), 1), (4, 1024, 256), dtype=_x0.dtype)
    del _x0
    return _d

def reference(L0_attn_x, L0_attn_Wq, L0_attn_bq, L0_attn_Wk, L0_attn_bk, L0_attn_Wv, L0_attn_bv, L0_attn_Wo, L0_attn_bo, L0_ffn_w_gate, L0_ffn_w_up, L0_ffn_w_down):

    def _L0_attn_ref(x, Wq, bq, Wk, bk, Wv, bv, Wo, bo):
        import jax, jax.numpy as jnp
        import numpy as np
        N_HEADS = 16
        D_HEAD = 128
        D_MODEL = 256
        MAXLEN = 256
        b, t, _ = x.shape
        h, dh = (N_HEADS, D_HEAD)
        scale = 1.0 / np.sqrt(dh).astype(np.float32)
        q = (x @ Wq + bq).reshape(b, h, t, dh)
        k = (x @ Wk + bk).reshape(b, t, h, dh).transpose(0, 2, 3, 1)
        v = (x @ Wv + bv).reshape(b, t, h, dh).transpose(0, 2, 1, 3)
        logits = jnp.einsum('bhtd,bhds->bhts', q, k) * scale
        mask = jnp.triu(jnp.full((t, t), -jnp.inf, dtype=x.dtype), k=1)
        weights = jax.nn.softmax(logits + mask, axis=-1)
        out = jnp.einsum('bhts,bhsd->bhtd', weights, v)
        out = out.transpose(0, 2, 1, 3).reshape(b, t, h * dh)
        return out @ Wo + bo

    def _L0_ffn_ref(x, w_gate, w_up, w_down):
        import jax, jax.numpy as jnp
        import numpy as np
        DIM_IN = 256
        DIM_HIDDEN = 1024
        gate = jnp.einsum('bsd,hd->bsh', x, w_gate)
        up = jnp.einsum('bsd,hd->bsh', x, w_up)
        gated = jax.nn.silu(gate) * up
        return jnp.einsum('bsh,dh->bsd', gated, w_down)
    x = L0_attn_x
    xn = _layernorm(x, axis=-1)
    x = x + _L0_attn_ref(xn, L0_attn_Wq, L0_attn_bq, L0_attn_Wk, L0_attn_bk, L0_attn_Wv, L0_attn_bv, L0_attn_Wo, L0_attn_bo) + _L0_ffn_ref(xn, L0_ffn_w_gate, L0_ffn_w_up, L0_ffn_w_down)
    return x

_drawn_inputs = setup_inputs


def setup_inputs(seed=0):
    import zlib

    import numpy as np

    out = dict(_drawn_inputs(seed))
    spreads = {'L0_attn_bq': (0.0, 0.8),
     'L0_attn_bk': (0.0, 0.8),
     'L0_attn_bv': (0.0, 0.1),
     'L0_attn_bo': (0.0, 0.1)}
    factors = {'L0_attn_Wq': 8.0, 'L0_attn_Wk': 8.0}
    for name, (base, spread) in spreads.items():
        noise = np.random.default_rng([zlib.crc32(name.encode()), seed]).standard_normal(out[name].shape)
        drawn = base * np.exp(spread * noise) if base else spread * noise
        out[name] = jnp.asarray(drawn.astype(out[name].dtype))
    for name, factor in factors.items():
        out[name] = (out[name] * factor).astype(out[name].dtype)
    return out
```

```python
from contextlib import ExitStack

import numpy as np

import concourse.bass as bass
from concourse import mybir

F32 = mybir.dt.float32
F32R = mybir.dt.float32r
BF16 = mybir.dt.bfloat16
ALU = mybir.AluOpType
ACT = mybir.ActivationFunctionType
AX_X = mybir.AxisListType.X

P = 128
B, T, D = 4, 1024, 256
NH, DH = 16, 128
HD = NH * DH
HID = 1024
KT = D // P
BANK = 512
EPS = 1e-5
SCALE = float(np.float32(1.0) / np.sqrt(np.float32(DH)))
MASKED = -1e30

CH = 512
NC = B * T // CH
CT = CH // P
NT = B * T // P
HT = HID // P

NHD = B * NH
NI = T // P
NG = NHD * NI
NK = NI // 2
QC = 2 * P
GROUP = 4
QTOK = T // NH
RQ = T // QTOK
T_LAG = 2
PV_LAG = 4
Y_LAG = 6
LAST = NG + Y_LAG

HILO = ((0, 0), (0, 1), (1, 0))

T_BANKS = [sum((j + 4) // 4 for j in range(i + 1)) for i in range(NI)]


def t_banks_through(g):
    return T_BANKS[-1] * (g // NI) + T_BANKS[g % NI] if g >= 0 else 0


def plan_pieces():
    before = [("Q", 0, m) for m in range(8)] + [("K", 0, 0), ("K", 0, 1)] + [("V", 0, m) for m in range(4)]
    early, late = {}, {}
    for n in range(NHD):
        r, pair, quad = n % 4, n // 2, n // 4
        e = {i: [] for i in range(NI)}
        l = {i: [] for i in range(NI)}
        batch_end = n % NH == NH - 1
        if n + 1 < NHD:
            at = {0: (1, 3), 1: (0, 2), 2: (1, 3), 3: (0, 1)}[r]
            e[at[0]].append(("K", n + 1, 0))
            e[at[1]].append(("K", n + 1, 1))
        if r == 1 and pair + 1 < NHD // 2:
            for m, i in enumerate((1, 3, 4, 5)):
                e[i].append(("V", pair + 1, m))
        if r == 2 and n % NH != NH - 2 and pair + 1 < NHD // 2:
            for m, (d, i) in enumerate(((e, 5), (e, 6), (e, 7), (l, 7))):
                d[i].append(("V", pair + 1, m))
        if r == 3 and quad + 1 < NHD // GROUP:
            for m in range(8):
                (e if m % 2 == 0 else l)[2 + m // 2].append(("Q", quad + 1, m))
        if batch_end and n + 1 < NHD:
            for m, (d, i) in enumerate(((l, 6), (e, 7), (l, 7), (l, 7))):
                d[i].append(("V", pair + 1, m))
        for i in range(NI):
            early[n * NI + i] = e[i]
            late[n * NI + i] = l[i]
    for pair in range(NHD // 2):
        for k in range(NK):
            g = (2 * pair + 1) * NI + 2 * k + Y_LAG
            early.setdefault(g, []).insert(0, ("y", pair, k))
    order = list(before)
    for g in range(LAST + 1):
        order += early.get(g, []) + late.get(g, [])
    number = {piece: j for j, piece in enumerate(order)}
    return before, early, late, order, number


def plan_splits():
    before = [("Wk", 0), ("Wv", 0), ("Wk", 1)]
    at = {}
    for n in range(NHD):
        r = n % 4
        if n + 2 < NHD:
            at.setdefault((n, 1), []).append(("Wk", n + 2))
        if r == 0:
            at.setdefault((n, 2), []).append(("Wv", n // 2 + 1))
        if r == 1 and n // 2 + 2 < NHD // 2:
            at.setdefault((n, 6), []).append(("Wv", n // 2 + 2))
        if r % 2 == 0:
            at.setdefault((n, 6), []).append(("Wo", n // 2))
    order = list(before)
    for key in sorted(at):
        order += at[key]
    return before, at, {s: j for j, s in enumerate(order)}


def attention_ffn_block(nc, x, Wq, bq, Wk, bk, Wv, bv, Wo, bo, w_gate, w_up, w_down, out):
    before, early, late, pieces, piece_no = plan_pieces()
    splits_before, splits_at, split_no = plan_splits()
    hi_count, c = {}, 0
    for piece in pieces:
        c += piece[0] in "KV"
        hi_count[piece] = c

    xnT_dram = nc.dram_tensor("xnT_dram", [B, 2, P, KT, T], F32, kind="Internal").ap()
    base_dram = nc.dram_tensor("base_dram", [B * T, D], F32, kind="Internal").ap()

    x_rows = x.rearrange("b t d -> (b t) d").rearrange("(n p) d -> p n d", p=P)
    base_rows = base_dram.rearrange("(n p) d -> p n d", p=P)
    out_rows = out.rearrange("b t d -> (b t) d").rearrange("(n p) d -> p n d", p=P)
    Wq_rows = Wq.rearrange("(k p) n -> p k n", p=P)
    Wk_rows = Wk.rearrange("(k p) n -> p k n", p=P)
    Wv_rows = Wv.rearrange("(k p) n -> p k n", p=P)
    Wo_rows = Wo.rearrange("(h p) n -> p h n", p=P)

    ctx = ExitStack()
    with ctx:
        def sb(name, shape, dt, where=ctx):
            return where.enter_context(nc.sbuf_tensor(name, shape, dt))

        def sb2(name, shape, where=ctx):
            return [sb(f"{name}_{part}", shape, F32R, where) for part in ("hi", "lo")]

        def sem(name):
            return ctx.enter_context(nc.semaphore(name))

        ident = sb("ident", [P, P], F32)
        ident_bf = sb("ident_bf", [P, P], BF16)
        mask_bf = sb("mask_bf", [P, P], BF16)
        bias_rows = sb("bias_rows", [3 * NH, P], F32)
        bias = sb("bias", [P, 3 * NH], F32)
        bqs_sb = sb("bqs_sb", [P, RQ], F32)
        bq_sb, bk_sb, bv_sb = (bias[:, j * NH:(j + 1) * NH] for j in range(3))

        a = ExitStack()
        raw_w = sb("raw_w", [P, 3 * KT * HID], F32, a)
        sil = sb("sil", [P, 2, CH], F32, a)
        y_stage = sb("y_stage", [P, 2, 2, D], F32, a)
        wgT = sb2("wgT", [P, KT, HID], a)
        wuT = sb2("wuT", [P, KT, HID], a)
        xnT_a = sb2("xnT_a", [P, 2, KT, CH], a)
        wdT = sb2("wdT", [P, HT, D], a)
        x_sb = sb("x_sb", [P, NT, D], F32, a)
        hid = sb2("hid", [P, 2, HT, CH], a)
        xn_sb = sb("xn_sb", [P, CT, D], F32, a)
        bo_sb = sb("bo_sb", [P, D], F32, a)
        stats = sb("stats", [P, 2, 6], F32, a)
        mean_var = sb("mean_var", [P, NT, 2], F32, a)
        var_eps = sb("var_eps", [P, NT], F32, a)
        std = sb("std", [P, NT], F32, a)
        rstd = sb("rstd", [P, NT], F32, a)
        newton = sb("newton", [P, NT], F32, a)
        a.close()
        wg_raw = raw_w[:, 0:KT * HID].rearrange("p (n d) -> p n d", d=D)
        wu_raw = raw_w[:, KT * HID:2 * KT * HID].rearrange("p (n d) -> p n d", d=D)
        wd_raw = raw_w[:, 2 * KT * HID:3 * KT * HID].rearrange("p (n h) -> p n h", h=HID)
        wq_raw = raw_w[:, 0:KT * HD].rearrange("p (k n) -> p k n", k=KT)

        v = sb2("v", [P, 2, NI, 2 * DH])
        wq = sb2("wq", [P, KT, HD])
        xnT = sb2("xnT", [P, KT, T])
        qT = sb("qT", [P, GROUP, T], F32)
        q = sb2("q", [P, 2, BANK])
        k = sb2("k", [P, 2, T])
        prob = sb("prob", [P, 3, T], F32)
        pT = [sb2("pT_even", [P, NI - 2, QC]), sb2("pT_odd", [P, NI, QC])]
        oT_even = sb2("oT_even", [P, T])
        oT_odd = sb2("oT_odd", [P, 2, QC])
        y = sb("y", [P, NI, D], F32)
        wk_raw = sb("wk_raw", [P, 2, KT, DH], F32)
        wk = sb2("wk", [P, 2, KT, DH])
        wv_raw = sb("wv_raw", [P, KT, 2 * DH], F32)
        wv = sb2("wv", [P, KT, 2 * DH])
        wo_raw = sb("wo_raw", [P, 2, D], F32)
        wo = sb2("wo", [P, 2, D])
        neg_max = sb("neg_max", [P, 4], F32)
        row_sum = sb("row_sum", [P, 4], F32)
        inv_sum = sb("inv_sum", [P, 4], F32)

        def pb(name, cols):
            return ctx.enter_context(nc.psum_tensor(name, [P, cols], F32))

        s_ps = [pb("s_ps0", 2 * BANK), pb("s_ps1", 2 * BANK)]
        t_ps = [pb("t_ps0", BANK), pb("t_ps1", BANK)]
        o_ps = pb("o_ps", BANK)
        m_ps = pb("m_ps", BANK)

        s_x = [sem(f"s_x{n}") for n in range(NC)]
        s_wg, s_wu, s_wd, s_wqraw = sem("s_wg"), sem("s_wu"), sem("s_wd"), sem("s_wqraw")
        s_bias, s_bo = sem("s_bias"), sem("s_bo")
        s_xst = [sem("s_xst0"), sem("s_xst1")]
        s_yst = [sem("s_yst0"), sem("s_yst1")]
        s_xload = [sem("s_xload_hi"), sem("s_xload_lo")]
        s_wkraw = [sem("s_wkraw0"), sem("s_wkraw1")]
        s_wvraw, s_woraw = sem("s_wvraw"), sem("s_woraw")
        s_base = [sem(f"s_base{j}") for j in range(NK)]
        s_out = [sem(f"s_out{j}") for j in range(NK)]
        s_const, s_biasT, s_bcol, s_bqs = sem("s_const"), sem("s_biasT"), sem("s_bcol"), sem("s_bqs")
        s_stat = sem("s_stat")
        s_veps = sem("s_veps")
        s_std = sem("s_std")
        s_xn = sem("s_xn")
        s_ta = sem("s_ta")
        s_tahi = sem("s_tahi")
        s_talo = sem("s_talo")
        s_gate, s_up = sem("s_gate"), sem("s_up")
        s_silu, s_h = sem("s_silu"), sem("s_h")
        s_hidhi, s_hid = sem("s_hidhi"), sem("s_hid")
        s_xbo = sem("s_xbo")
        s_down = sem("s_down")
        s_ffn = sem("s_ffn")
        s_wqhi, s_wq = sem("s_wqhi"), sem("s_wq")
        s_qk = sem("s_qk")
        s_max = sem("s_max")
        s_exp = sem("s_exp")
        s_inv = sem("s_inv")
        s_norm = sem("s_norm")
        s_t = sem("s_t")
        s_thi, s_tlo = sem("s_thi"), sem("s_tlo")
        s_pv = sem("s_pv")
        s_ohi, s_olo = sem("s_ohi"), sem("s_olo")
        s_fill = sem("s_fill")
        s_fillhi = sem("s_fillhi")
        s_piece = sem("s_piece")
        s_qhi, s_q = sem("s_qhi"), sem("s_q")
        s_splithi, s_split = sem("s_splithi"), sem("s_split")

        def waits(eng):
            seen = {}

            def need(s, count):
                if count > seen.get(id(s), 0):
                    seen[id(s)] = count
                    eng.wait_ge(s, count)
            return need

        a_banks = [("wg", j) for j in range(4)] + [("x", 0, kt) for kt in range(KT)]
        a_banks += [("wu", j) for j in range(4)] + [("wd", j) for j in range(4)]
        a_banks += [("x", c, kt) for c in range(1, NC) for kt in range(KT)]
        a_bank_no = {b: j for j, b in enumerate(a_banks)}

        def a_dst(b, part):
            if b[0] == "x":
                return xnT_a[part][:, b[1] % 2, b[2], :]
            if b[0] == "wd":
                return wdT[part][:, 2 * b[1]:2 * b[1] + 2, :].rearrange("p n d -> p (n d)")
            kt, half = divmod(b[1], 2)
            return (wgT if b[0] == "wg" else wuT)[part][:, kt, half * BANK:(half + 1) * BANK]

        def o_slot(n, kc):
            if n % 2 == 0:
                return ([t[:, kc * QC:(kc + 1) * QC] for t in oT_even], ("y", n // 2 - 1, kc) if n >= 2 else None)
            j = (n // 2) * NK + kc - 2
            return ([t[:, kc % 2, :] for t in oT_odd], ("y", j // NK, j % NK) if j >= 0 else None)

        std_groups = [(0, 1), (1, 2), (2, NC)]

        block = ctx.enter_context(nc.Block())

        @block.sync
        def _(eng):
            need = waits(eng)

            def load_x(c):
                eng.dma_start(x_sb[:, c * CT:(c + 1) * CT, :], x_rows[:, c * CT:(c + 1) * CT, :]).then_inc(s_x[c], 16)

            load_x(0)
            eng.dma_start(wg_raw, w_gate.rearrange("(n p) d -> p n d", p=P)).then_inc(s_wg, 16)
            eng.dma_start(wu_raw, w_up.rearrange("(n p) d -> p n d", p=P)).then_inc(s_wu, 16)
            load_x(1)
            eng.dma_start(wd_raw, w_down.rearrange("(n p) h -> p n h", p=P)).then_inc(s_wd, 16)
            eng.dma_start(bo_sb[:, :], bo.partition_broadcast(P)).then_inc(s_bo, 16)
            for c in range(2, NC):
                load_x(c)
            for j, src in enumerate((bq, bk, bv)):
                eng.dma_start(bias_rows[j * NH:(j + 1) * NH, :], src.rearrange("(h p) -> h p", p=P)).then_inc(s_bias, 16)

            def store_xnT(c):
                need(s_talo, a_bank_no[("x", c, KT - 1)] + 1)
                b, half = divmod(c, T // CH)
                for part in range(2):
                    eng.dma_start(xnT_dram[b, part][:, :, half * CH:(half + 1) * CH],
                                  xnT_a[part][:, c % 2, :, :].bitcast(F32)).then_inc(s_xst[c % 2], 16)

            def store_base(c):
                for d in range(2):
                    need(s_ffn, 2 * c + d + 1)
                    t0 = c * CT + 2 * d
                    eng.dma_start(base_rows[:, t0:t0 + 2, :], y_stage[:, d, :, :]).then_inc(s_yst[d], 16)

            store_xnT(0)
            for c in range(NC):
                if c + 1 < NC:
                    store_xnT(c + 1)
                if c == 0:
                    need(s_ta, a_bank_no[("wd", 3)] + 1)
                    eng.dma_start(wq_raw, Wq_rows).then_inc(s_wqraw, 16)
                if c >= 1:
                    store_base(c - 1)

            def load_xnT(b):
                for part in range(2):
                    eng.dma_start(xnT[part][:, :, :].bitcast(F32), xnT_dram[b, part]).then_inc(s_xload[part], 16)

            need(s_up, NC * HT)
            for slot in range(2):
                need(s_xst[slot], 32 * (NC // 2))
            load_xnT(0)
            store_base(NC - 1)
            need(s_down, 2 * NC)
            need(s_ffn, 2 * NC)

            def load_wk(n):
                h = n % NH
                if n >= 2:
                    need(s_split, split_no[("Wk", n - 2)] + 1)
                eng.dma_start(wk_raw[:, n % 2, :, :], Wk_rows[:, :, h * DH:(h + 1) * DH]).then_inc(s_wkraw[n % 2], 16)

            def load_wv(pair):
                h = 2 * pair % NH
                if pair >= 1:
                    need(s_split, split_no[("Wv", pair - 1)] + 1)
                eng.dma_start(wv_raw[:, :, :], Wv_rows[:, :, h * DH:(h + 2) * DH]).then_inc(s_wvraw, 16)

            def load_wo(pair):
                h = 2 * pair % NH
                if pair >= 1:
                    need(s_split, split_no[("Wo", pair - 1)] + 1)
                eng.dma_start(wo_raw[:, :, :], Wo_rows[:, h:h + 2, :]).then_inc(s_woraw, 16)

            def load_base(b, j):
                if b >= 1:
                    need(s_out[j], 16 * b)
                t0 = b * NI + 2 * j
                eng.dma_start(y[:, 2 * j:2 * j + 2, :], base_rows[:, t0:t0 + 2, :]).then_inc(s_base[j], 16)

            def store_out(b, j):
                need(s_piece, piece_no[("y", (b + 1) * NH // 2 - 1, j)] + 1)
                t0 = b * NI + 2 * j
                eng.dma_start(out_rows[:, t0:t0 + 2, :], y[:, 2 * j:2 * j + 2, :]).then_inc(s_out[j], 16)

            load_wk(0)
            load_wv(0)
            load_wk(1)
            load_wo(0)
            for slot in range(2):
                need(s_yst[slot], 16 * NC)
            for j in range(NK):
                load_base(0, j)
            for n in range(NHD):
                r, b = n % 4, n // NH
                if n + 2 < NHD:
                    load_wk(n + 2)
                if r == 0:
                    load_wv(n // 2 + 1)
                if r == 1 and n // 2 + 2 < NHD // 2:
                    load_wv(n // 2 + 2)
                if r % 2 == 0 and n:
                    load_wo(n // 2)
                if n % NH == 0 and n:
                    for j in range(NK):
                        store_out(b - 1, j)
                        load_base(b, j)
                if n % NH == NH - 2 and b + 1 < B:
                    need(s_fill, piece_no[("K", n + 1, 1)] + 1)
                    load_xnT(b + 1)
            for j in range(NK):
                store_out(B - 1, j)
            for j in range(NK):
                need(s_out[j], 16 * B)

        @block.gpsimd
        def _(eng):
            need = waits(eng)
            eng.memset(ident[:, :], 0.0).then_inc(s_const, 1)
            eng.memset(mask_bf[:, :], 0.0).then_inc(s_const, 1)
            need(s_const, 2)
            eng.affine_select(out=ident[:, :], in_=ident[:, :], compare_op=ALU.not_equal, fill=1.0,
                              base=0, pattern=[[-1, P]], channel_multiplier=1).then_inc(s_const, 1)
            eng.affine_select(out=mask_bf[:, :], in_=mask_bf[:, :], compare_op=ALU.is_ge, fill=MASKED,
                              base=0, pattern=[[-1, P]], channel_multiplier=1).then_inc(s_const, 1)
            need(s_const, 4)
            eng.tensor_copy(ident_bf[:, :], ident[:, :]).then_inc(s_const, 1)

            count = {}

            def split(dst, src, sem_hi, sem_lo, index):
                count[id(sem_hi)] = count.get(id(sem_hi), 0) + 1
                eng.tensor_scalar(index(dst[0]), src, 1.0, 1.0, ALU.mult, ALU.mult).then_inc(sem_hi, 1)
                need(sem_hi, count[id(sem_hi)])
                eng.tensor_tensor(index(dst[1]), src, index(dst[0]), ALU.subtract).then_inc(sem_lo, 1)

            for c in range(NC):
                for ht in range(HT):
                    u = c * HT + ht
                    if ht == 0:
                        need(s_xn, c + 1)
                        need(s_bo, 16)
                        for t in range(c * CT, (c + 1) * CT):
                            ins = eng.tensor_tensor(x_sb[:, t, :], x_sb[:, t, :], bo_sb[:, :], ALU.add)
                        ins.then_inc(s_xbo, 1)
                        if c >= 2:
                            need(s_down, 2 * (c - 1))
                    need(s_h, u + 1)
                    split(hid, sil[:, u % 2, :], s_hidhi, s_hid, lambda t: t[:, c % 2, ht, :])

            need(s_wqraw, 16)
            need(s_up, NC * HT)
            for kt in range(KT):
                for half in range(2):
                    cols = slice(half * HD // 2, (half + 1) * HD // 2)
                    split(wq, wq_raw[:, kt, cols], s_wqhi, s_wq, lambda t: t[:, kt, cols])
            need(s_down, 2 * NC)
            need(s_ffn, 2 * NC)

            def split_weight(which):
                what, j = which
                if what == "Wk":
                    need(s_wkraw[j % 2], 16 * (j // 2 + 1))
                    if j >= 2:
                        need(s_fill, piece_no[("K", j - 2, 1)] + 1)
                    split(wk, wk_raw[:, j % 2, :, :], s_splithi, s_split, lambda t: t[:, j % 2, :, :])
                elif what == "Wv":
                    need(s_wvraw, 16 * (j + 1))
                    if j:
                        need(s_fill, piece_no[("V", j - 1, 3)] + 1)
                    split(wv, wv_raw[:, :, :], s_splithi, s_split, lambda t: t[:, :, :])
                else:
                    need(s_woraw, 16 * (j + 1))
                    if j:
                        need(s_fill, piece_no[("y", j - 1, NK - 1)] + 1)
                    split(wo, wo_raw[:, :, :], s_splithi, s_split, lambda t: t[:, :, :])

            def split_q(n, half):
                need(s_piece, piece_no[("Q", n // GROUP, 7)] + 1)
                if n:
                    need(s_qk, NI * (n - 1) + 4 * (half + 1))
                split(q, qT[:, n % GROUP, half * BANK:(half + 1) * BANK], s_qhi, s_q, lambda t: t[:, half, :])

            for which in splits_before:
                split_weight(which)
            split_q(0, 0)
            for g in range(NG + 1):
                if g >= 1:
                    j, L = g - 1, ((g - 1) % NI + 1) * P
                    need(s_inv, j + 1)
                    eng.tensor_scalar(prob[:, j % 3, 0:L], prob[:, j % 3, 0:L], inv_sum[:, j % 4:j % 4 + 1], 1.0,
                                      ALU.mult, ALU.mult).then_inc(s_norm, 1)
                if g == NG:
                    break
                n, i = divmod(g, NI)
                if i == 0:
                    split_q(n, 1)
                for which in splits_at.get((n, i), []):
                    split_weight(which)
                if i == (7 if n % GROUP == GROUP - 1 else 5) and n + 1 < NHD:
                    split_q(n + 1, 0)

        @block.scalar
        def _(eng):
            need = waits(eng)

            def roots(j):
                t0, t1 = std_groups[j][0] * CT, std_groups[j][1] * CT
                need(s_veps, j + 1)
                eng.activation(std[:, t0:t1], var_eps[:, t0:t1], ACT.Sqrt).then_inc(s_std, 1)

            def part_hi(b):
                j = a_bank_no[b]
                need(s_ta, j + 1)
                if b[0] == "x" and b[1] >= 2:
                    need(s_up, (b[1] - 1) * HT)
                    need(s_xst[b[1] % 2], 32 * (b[1] // 2))
                eng.activation(a_dst(b, 0), t_ps[j % 2][:, :], ACT.Copy).then_inc(s_tahi, 1)

            roots(0)
            for b in a_banks[:10]:
                part_hi(b)
            for c in range(NC):
                for ht in range(HT):
                    u = c * HT + ht
                    need(s_gate, u + 1)
                    if u >= 2:
                        need(s_hid, u - 1)
                    eng.activation(sil[:, u % 2, :], s_ps[u % 2][:, 0:CH], ACT.Silu).then_inc(s_silu, 1)
                    if ht == 1 and c + 1 < len(std_groups):
                        roots(c + 1)
                    if ht == 3:
                        if c == 0:
                            for b in a_banks[10:14]:
                                part_hi(b)
                        if c + 1 < NC:
                            for kt in range(KT):
                                part_hi(("x", c + 1, kt))

            need(s_biasT, 1)
            eng.activation(bias[:, :], t_ps[0][:, 0:3 * NH], ACT.Copy).then_inc(s_bcol, 1)
            need(s_bcol, 1)
            eng.activation(bqs_sb[:, :], bq_sb, ACT.Copy, scale=SCALE).then_inc(s_bqs, 1)
            need(s_bqs, 1)
            need(s_ffn, 2 * NC)
            need(s_hid, NC * HT)
            for slot in range(2):
                need(s_yst[slot], 16 * NC)

            def piece_out(piece):
                what, j, m = piece
                if what == "y":
                    return
                need(s_fill, piece_no[piece] + 1)
                if what == "K":
                    if j >= 2:
                        need(s_qk, NI * (j - 1))
                    h = j % NH
                    eng.activation(k[0][:, j % 2, m * BANK:(m + 1) * BANK], m_ps[:, :], ACT.Identity,
                                   bias=bk_sb[:, h:h + 1]).then_inc(s_fillhi, 1)
                elif what == "V":
                    need(s_wq, 4)
                    if j >= 2:
                        need(s_pv, NK * 2 * (j - 1))
                    eng.activation(v[0][:, j % 2, 2 * m:2 * m + 2, :].rearrange("p n d -> p (n d)"), m_ps[:, :],
                                   ACT.Copy).then_inc(s_fillhi, 1)
                else:
                    if j:
                        need(s_q, 2 * GROUP * j)
                    for c2 in range(2):
                        c = 2 * m + c2
                        dst = qT[:, :, :].rearrange("p h (r c) -> p c h r", c=RQ)[:, c]
                        src = m_ps[:, c2 * QC:(c2 + 1) * QC].rearrange("p (h r) -> p h r", h=GROUP)
                        ins = eng.activation(dst, src, ACT.Identity, bias=bqs_sb[:, c:c + 1], scale=SCALE)
                    ins.then_inc(s_piece, 1)

            for piece in before:
                piece_out(piece)
            for g in range(LAST + 1):
                if g < NG:
                    L = (g % NI + 1) * P
                    need(s_max, g + 1)
                    if g >= 3:
                        need(s_t, t_banks_through(g - 3))
                    eng.activation(prob[:, g % 3, 0:L], s_ps[g % 2][:, 0:L], ACT.Exp,
                                   bias=neg_max[:, g % 4:g % 4 + 1],
                                   accum_out=row_sum[:, g % 4:g % 4 + 1]).then_inc(s_exp, 1)
                for piece in early.get(g, []):
                    piece_out(piece)
                j = g - T_LAG
                if 0 <= j < NG:
                    n, i = divmod(j, NI)
                    kc = i // 2
                    ck = n * NK + kc
                    if ck >= 2:
                        need(s_pv, ck - 1)
                    for bank in range((i + 4) // 4):
                        tb = t_banks_through(j - 1) + bank
                        k0, k1 = 4 * bank, min(4 * bank + 4, i + 1)
                        need(s_t, tb + 1)
                        eng.activation(pT[kc % 2][0][:, k0:k1, (i % 2) * P:(i % 2 + 1) * P],
                                       t_ps[tb % 2][:, 0:(k1 - k0) * P].rearrange("p (n t) -> p n t", t=P),
                                       ACT.Copy).then_inc(s_thi, 1)
                j = g - PV_LAG
                if 0 <= j < NG and j % 2 == 1:
                    n, kc = j // NI, (j % NI) // 2
                    ck = n * NK + kc
                    need(s_pv, ck + 1)
                    dst, last_read = o_slot(n, kc)
                    if last_read:
                        need(s_fill, piece_no[last_read] + 1)
                    h = n % NH
                    eng.activation(dst[0], o_ps[:, 0:QC], ACT.Identity, bias=bv_sb[:, h:h + 1]).then_inc(s_ohi, 1)
                for piece in late.get(g, []):
                    piece_out(piece)

        @block.vector
        def _(eng):
            need = waits(eng)
            chain = [0]

            def link(ins):
                chain[0] += 1
                ins.then_inc(s_stat, 1)
                need(s_stat, chain[0])

            def statistics(c):
                need(s_x[c], 16)
                for t in range(c * CT, (c + 1) * CT):
                    link(eng.bn_stats(stats[:, t % 2, :], x_sb[:, t, :]))
                    link(eng.bn_aggr(mean_var[:, t, :], stats[:, t % 2, :]))

            def plus_eps(j):
                t0, t1 = std_groups[j][0] * CT, std_groups[j][1] * CT
                eng.tensor_scalar(var_eps[:, t0:t1], mean_var[:, t0:t1, 1], EPS, None, ALU.add).then_inc(s_veps, 1)

            def inverse_std(j):
                t0, t1 = std_groups[j][0] * CT, std_groups[j][1] * CT
                r, w, s = rstd[:, t0:t1], newton[:, t0:t1], var_eps[:, t0:t1]
                need(s_veps, j + 1)
                need(s_std, j + 1)
                link(eng.reciprocal(r, std[:, t0:t1]))
                link(eng.tensor_tensor(w, r, r, ALU.mult))
                link(eng.tensor_tensor(w, w, s, ALU.mult))
                link(eng.tensor_scalar(w, w, -0.5, 1.5, ALU.mult, ALU.add))
                link(eng.tensor_tensor(r, r, w, ALU.mult))

            def normed(c):
                if c:
                    need(s_ta, a_bank_no[("x", c - 1, KT - 1)] + 1)
                for j in range(CT):
                    t = c * CT + j
                    ins = eng.tensor_scalar(xn_sb[:, j, :], x_sb[:, t, :], mean_var[:, t, 0:1], rstd[:, t:t + 1],
                                            ALU.subtract, ALU.mult)
                ins.then_inc(s_xn, 1)

            def part_lo(b):
                j = a_bank_no[b]
                need(s_tahi, j + 1)
                eng.tensor_tensor(a_dst(b, 1), t_ps[j % 2][:, :], a_dst(b, 0), ALU.subtract).then_inc(s_talo, 1)

            def base_out(c):
                need(s_xbo, c + 1)
                for d in range(2):
                    need(s_down, 2 * c + d + 1)
                    if c:
                        need(s_yst[d], 16 * c)
                    t0 = c * CT + 2 * d
                    eng.tensor_tensor(y_stage[:, d, :, :].rearrange("p n d -> p (n d)"), (o_ps, m_ps)[d][:, :],
                                      x_sb[:, t0:t0 + 2, :].rearrange("p n d -> p (n d)"), ALU.add).then_inc(s_ffn, 1)

            statistics(0)
            plus_eps(0)
            inverse_std(0)
            normed(0)
            for b in a_banks[:10]:
                part_lo(b)
            for c in range(NC):
                for ht in range(HT):
                    u = c * HT + ht
                    if c == 0 and ht == 1:
                        statistics(1)
                        plus_eps(1)
                    if c == 0 and ht >= 3:
                        statistics(ht - 1)
                    if c == 1 and ht == 0:
                        statistics(NC - 1)
                        plus_eps(2)
                    need(s_up, u + 1)
                    need(s_silu, u + 1)
                    eng.tensor_tensor(sil[:, u % 2, :], sil[:, u % 2, :], s_ps[u % 2][:, CH:2 * CH], ALU.mult)\
                       .then_inc(s_h, 1)
                    if ht == 1 and c + 1 < len(std_groups):
                        inverse_std(c + 1)
                    if ht == 2 and c + 1 < NC:
                        normed(c + 1)
                    if ht == 3:
                        if c == 0:
                            for b in a_banks[10:14]:
                                part_lo(b)
                        if c + 1 < NC:
                            for kt in range(KT):
                                part_lo(("x", c + 1, kt))
                if c >= 1:
                    base_out(c - 1)
            base_out(NC - 1)

            need(s_bcol, 1)
            need(s_hid, NC * HT)
            for slot in range(2):
                need(s_yst[slot], 16 * NC)

            def piece_out(piece):
                what, j, m = piece
                if what == "Q":
                    return
                if what == "y":
                    b, pair = divmod(j, NH // 2)
                    need(s_fill, piece_no[piece] + 1)
                    need(s_base[m], 16 * (b + 1))
                    if pair:
                        need(s_piece, piece_no[("y", j - 1, m)] + 1)
                    rows = y[:, 2 * m:2 * m + 2, :].rearrange("p n d -> p (n d)")
                    eng.tensor_tensor(rows, m_ps[:, :], rows, ALU.add).then_inc(s_piece, 1)
                    return
                need(s_fillhi, hi_count[piece])
                if what == "K":
                    h, cols = j % NH, slice(m * BANK, (m + 1) * BANK)
                    eng.scalar_tensor_tensor(out=k[1][:, j % 2, cols], in0=m_ps[:, :], scalar=bk_sb[:, h:h + 1],
                                             in1=k[0][:, j % 2, cols], op0=ALU.add, op1=ALU.subtract)\
                       .then_inc(s_piece, 1)
                else:
                    hi, lo = (t[:, j % 2, 2 * m:2 * m + 2, :].rearrange("p n d -> p (n d)") for t in v)
                    eng.tensor_tensor(lo, m_ps[:, :], hi, ALU.subtract).then_inc(s_piece, 1)

            for piece in before:
                piece_out(piece)
            for g in range(LAST + 1):
                if g < NG:
                    need(s_qk, g + 1)
                    if g >= 4:
                        need(s_exp, g - 3)
                    L = (g % NI + 1) * P
                    eng.tensor_reduce(neg_max[:, g % 4:g % 4 + 1], s_ps[g % 2][:, 0:L], AX_X, ALU.max,
                                      negate=True).then_inc(s_max, 1)
                if 1 <= g <= NG:
                    j = g - 1
                    need(s_exp, j + 1)
                    if j >= 4:
                        need(s_norm, j - 3)
                    eng.reciprocal(inv_sum[:, j % 4:j % 4 + 1], row_sum[:, j % 4:j % 4 + 1]).then_inc(s_inv, 1)
                for piece in early.get(g, []):
                    piece_out(piece)
                j = g - T_LAG
                if 0 <= j < NG:
                    n, i = divmod(j, NI)
                    kc = i // 2
                    for bank in range((i + 4) // 4):
                        tb = t_banks_through(j - 1) + bank
                        k0, k1 = 4 * bank, min(4 * bank + 4, i + 1)
                        need(s_thi, tb + 1)
                        hi, lo = (t[:, k0:k1, (i % 2) * P:(i % 2 + 1) * P] for t in pT[kc % 2])
                        eng.tensor_tensor(lo, t_ps[tb % 2][:, 0:(k1 - k0) * P].rearrange("p (n t) -> p n t", t=P), hi,
                                          ALU.subtract).then_inc(s_tlo, 1)
                j = g - PV_LAG
                if 0 <= j < NG and j % 2 == 1:
                    n, kc = j // NI, (j % NI) // 2
                    need(s_ohi, n * NK + kc + 1)
                    dst, _ = o_slot(n, kc)
                    h = n % NH
                    eng.scalar_tensor_tensor(out=dst[1], in0=o_ps[:, 0:QC], scalar=bv_sb[:, h:h + 1], in1=dst[0],
                                             op0=ALU.add, op1=ALU.subtract).then_inc(s_olo, 1)
                for piece in late.get(g, []):
                    piece_out(piece)

        @block.tensor
        def _(eng):
            need = waits(eng)

            def product(dst, terms):
                for j, (sta, mov) in enumerate(terms):
                    for s, m in HILO:
                        ins = eng.matmul(dst, sta[s], mov[m], start=(j == 0 and (s, m) == HILO[0]),
                                         stop=(j == len(terms) - 1 and (s, m) == HILO[-1]))
                return ins

            def parts(t, index):
                return [index(t[0]), index(t[1])]

            def transposes(b):
                j = a_bank_no[b]
                need(s_const, 3)
                if b[0] == "x":
                    need(s_xn, b[1] + 1)
                    src = [xn_sb[:, t, b[2] * P:(b[2] + 1) * P] for t in range(CT)]
                elif b[0] == "wd":
                    need(s_wd, 16)
                    src = [wd_raw[:, dt, ht * P:(ht + 1) * P] for ht in (2 * b[1], 2 * b[1] + 1) for dt in range(KT)]
                else:
                    need(s_wg if b[0] == "wg" else s_wu, 16)
                    kt, half = divmod(b[1], 2)
                    raw = wg_raw if b[0] == "wg" else wu_raw
                    src = [raw[:, 4 * half + ht, kt * P:(kt + 1) * P] for ht in range(4)]
                if j >= 2:
                    need(s_talo, j - 1)
                for c, s in enumerate(src):
                    ins = eng.transpose(t_ps[j % 2][:, c * P:(c + 1) * P], s, ident[:, :])
                ins.then_inc(s_ta, 1)

            def gate_up(c, ht):
                u = c * HT + ht
                need(s_talo, a_bank_no[("x", c, KT - 1)] + 1)
                if u == 0:
                    need(s_talo, a_bank_no[("wu", 3)] + 1)
                if u >= 2:
                    need(s_h, u - 1)
                for w, half, done in ((wgT, 0, s_gate), (wuT, 1, s_up)):
                    terms = [(parts(w, lambda t: t[:, kt, ht * P:(ht + 1) * P]),
                              parts(xnT_a, lambda t: t[:, c % 2, kt, :])) for kt in range(KT)]
                    product(s_ps[u % 2][:, half * CH:(half + 1) * CH], terms).then_inc(done, 1)

            def down(c):
                need(s_talo, a_bank_no[("wd", 3)] + 1)
                need(s_hid, (c + 1) * HT)
                for d in range(2):
                    if c:
                        need(s_ffn, 2 * (c - 1) + d + 1)
                    for t2 in range(2):
                        t = 2 * d + t2
                        terms = [(parts(hid, lambda h: h[:, c % 2, ht, t * P:(t + 1) * P]),
                                  parts(wdT, lambda w: w[:, ht, :])) for ht in range(HT)]
                        ins = product((o_ps, m_ps)[d][:, t2 * D:(t2 + 1) * D], terms)
                    ins.then_inc(s_down, 1)

            for b in a_banks[:10]:
                transposes(b)
            for c in range(NC):
                for ht in range(HT):
                    gate_up(c, ht)
                    if ht == 3:
                        if c == 0:
                            for b in a_banks[10:14]:
                                transposes(b)
                        if c + 1 < NC:
                            for kt in range(KT):
                                transposes(("x", c + 1, kt))
                if c >= 1:
                    down(c - 1)
            down(NC - 1)

            need(s_bias, 48)
            need(s_talo, len(a_banks))
            eng.transpose(t_ps[0][:, 0:3 * NH], bias_rows[:, :], ident[0:3 * NH, 0:3 * NH]).then_inc(s_biasT, 1)
            need(s_ffn, 2 * NC)
            need(s_const, 5)

            def issue_piece(piece):
                what, j, m = piece
                need(s_piece, piece_no[piece])
                if what == "y":
                    need(s_split, split_no[("Wo", j)] + 1)
                    need(s_olo, NK * (2 * j + 1) + m + 1)
                    for t2 in range(2):
                        even = parts(oT_even, lambda t: t[:, (2 * m + t2) * P:(2 * m + t2 + 1) * P])
                        odd = parts(oT_odd, lambda t: t[:, m % 2, t2 * P:(t2 + 1) * P])
                        terms = [(o, parts(wo, lambda t: t[:, hh, :])) for hh, o in enumerate((even, odd))]
                        ins = product(m_ps[:, t2 * D:(t2 + 1) * D], terms)
                    ins.then_inc(s_fill, 1)
                    return
                heads_per = {"K": 1, "V": 2, "Q": GROUP}[what]
                for part in range(2):
                    need(s_xload[part], 16 * (j * heads_per // NH + 1))
                if what == "K":
                    need(s_split, split_no[("Wk", j)] + 1)
                    terms = [(parts(wk, lambda t: t[:, j % 2, kt, :]),
                              parts(xnT, lambda t: t[:, kt, m * BANK:(m + 1) * BANK])) for kt in range(KT)]
                    ins = product(m_ps[:, :], terms)
                elif what == "V":
                    need(s_split, split_no[("Wv", j)] + 1)
                    for t2 in range(2):
                        st = 2 * m + t2
                        terms = [(parts(xnT, lambda t: t[:, kt, st * P:(st + 1) * P]),
                                  parts(wv, lambda t: t[:, kt, :])) for kt in range(KT)]
                        ins = product(m_ps[:, t2 * 2 * DH:(t2 + 1) * 2 * DH], terms)
                else:
                    need(s_wq, 4)
                    tok = j * GROUP % NH * QTOK
                    for c2 in range(2):
                        c = 2 * m + c2
                        terms = [(parts(wq, lambda t: t[:, kt, c * P:(c + 1) * P]),
                                  parts(xnT, lambda t: t[:, kt, tok:tok + QC])) for kt in range(KT)]
                        ins = product(m_ps[:, c2 * QC:(c2 + 1) * QC], terms)
                ins.then_inc(s_fill, 1)

            def scores(g):
                n, i = divmod(g, NI)
                need(s_piece, piece_no[("K", n, 1)] + 1)
                need(s_q, 2 * n + i // 4 + 1)
                if g >= 2:
                    need(s_exp, g - 1)
                L = (i + 1) * P
                qi = parts(q, lambda t: t[:, i // 4, (i % 4) * P:(i % 4 + 1) * P])
                for c0 in range(0, L, BANK):
                    c1 = min(c0 + BANK, L)
                    ki = parts(k, lambda t: t[:, n % 2, c0:c1])
                    for s, m in HILO:
                        ins = eng.matmul(s_ps[g % 2][:, c0:c1], qi[s], ki[m], start=(s, m) == HILO[0],
                                         stop=(c1 < L and (s, m) == HILO[-1]))
                eng.matmul(s_ps[g % 2][:, L - P:L], ident_bf[:, :], mask_bf[:, :], start=False, stop=True)\
                   .then_inc(s_qk, 1)

            def transpose_weights(g):
                i = g % NI
                need(s_norm, g + 1)
                for bank in range((i + 4) // 4):
                    tb = t_banks_through(g - 1) + bank
                    if tb == 0:
                        need(s_bcol, 1)
                    if tb >= 2:
                        need(s_tlo, tb - 1)
                    for kt in range(4 * bank, min(4 * bank + 4, i + 1)):
                        ins = eng.transpose(t_ps[tb % 2][:, (kt % 4) * P:(kt % 4 + 1) * P],
                                            prob[:, g % 3, kt * P:(kt + 1) * P], ident[:, :])
                    ins.then_inc(s_t, 1)

            def weights_times_v(n, kc, second):
                ck = n * NK + kc
                need(s_tlo, t_banks_through(n * NI + 2 * kc + 1))
                need(s_piece, piece_no[("V", n // 2, 3)] + 1)
                need(s_olo, ck)
                last = 2 * kc + 1
                for kt in range(kc + 1, last + 1) if second else range(kc + 1):
                    c0 = P if kt == last else 0
                    vi = parts(v, lambda t: t[:, n // 2 % 2, kt, (n % 2) * DH:(n % 2 + 1) * DH])
                    pi = parts(pT[kc % 2], lambda t: t[:, kt, c0:QC])
                    for s, m in HILO:
                        ins = eng.matmul(o_ps[:, c0:QC], vi[s], pi[m], start=(kt == 0 and (s, m) == HILO[0]),
                                         stop=(kt == last and (s, m) == HILO[-1]))
                if second:
                    ins.then_inc(s_pv, 1)

            for piece in before:
                issue_piece(piece)
            for g in range(LAST + 1):
                if g < NG:
                    scores(g)
                for piece in early.get(g, []):
                    issue_piece(piece)
                if 0 <= g - T_LAG < NG:
                    transpose_weights(g - T_LAG)
                j = g - PV_LAG
                if 0 <= j < NG:
                    weights_times_v(j // NI, (j % NI) // 2, j % 2 == 1)
                for piece in late.get(g, []):
                    issue_piece(piece)


_INS = ["L0_attn_x", "L0_attn_Wq", "L0_attn_bq", "L0_attn_Wk", "L0_attn_bk", "L0_attn_Wv", "L0_attn_bv",
        "L0_attn_Wo", "L0_attn_bo", "L0_ffn_w_gate", "L0_ffn_w_up", "L0_ffn_w_down"]


def kernel(**inputs):
    import concourse.bacc as bacc
    from concourse.bass_utils import run_bass_kernel_spmd

    nc = bacc.Bacc("TRN2", target_bir_lowering=False, num_devices=1)
    arrays, args = {}, []
    for name in _INS:
        arr = np.ascontiguousarray(inputs[name])
        arrays[f"in_{name}"] = arr
        args.append(nc.dram_tensor(f"in_{name}", arr.shape, mybir.dt.from_np(arr.dtype), kind="ExternalInput").ap())
    out = nc.dram_tensor("out_0", (B, T, D), F32, kind="ExternalOutput").ap()
    attention_ffn_block(nc, *args, out)
    r = run_bass_kernel_spmd(nc, [arrays], core_ids=[0])
    return r.results[0]["out_0"]
```

```python
from contextlib import ExitStack

import numpy as np

import concourse.bass as bass
from concourse import mybir

F32 = mybir.dt.float32
F32R = mybir.dt.float32r
ALU = mybir.AluOpType
ACT = mybir.ActivationFunctionType
AX_X = mybir.AxisListType.X

P = 128
B, T, D = 4, 1024, 256
NH, DH = 16, 128
HD = NH * DH
HID = 1024
KT = D // P
BANK = 512
EPS = 1e-5
SCALE = float(np.float32(1.0) / np.sqrt(np.float32(DH)))
MASKED = -1e30

CH = 512
NC = B * T // CH
CT = CH // P
NT = B * T // P
HT = HID // P

NHD = B * NH
NI = T // P
NG = NHD * NI
NK = NI // 2
QC = 2 * P
GROUP = 4
QTOK = T // NH
RQ = T // QTOK
T_LAG = 2
PV_LAG = 5
Y_LAG = 7
LAST = NG + Y_LAG

HILO = ((0, 0), (0, 1), (1, 0))

T_BANKS = [sum((j + 4) // 4 for j in range(i + 1)) for i in range(NI)]


def t_banks_through(g):
    return T_BANKS[-1] * (g // NI) + T_BANKS[g % NI] if g >= 0 else 0


def score_cols(i):
    L = (i + 1) * P
    c0 = 0 if L <= BANK else BANK - L // 2
    return c0, c0 + L


def plan_pieces():
    before = [("Q", 0, m) for m in range(8)] + [("K", 0, 0), ("K", 0, 1)] + [("V", 0, m) for m in range(4)]
    early = {g: [] for g in range(LAST + 1)}
    late = {g: [] for g in range(LAST + 1)}
    for pair in range(NHD // 2):
        for kc in range(NK):
            late[(2 * pair + 1) * NI + 2 * kc + Y_LAG].append(("y", pair, kc))
    for n in range(NHD - 1):
        r, pair, quad = n % 4, n // 2, n // GROUP

        def put(what, j, places, first=0):
            for m, (d, i) in enumerate(places, first):
                d[n * NI + i].append((what, j, m))

        put("K", n + 1, ((early, 0), (late, 0)) if r == 3 else ((early, 1), (early, 3)))
        if r == 0:
            put("V", pair + 1, ((early, 4), (early, 7)))
        if r == 1:
            put("V", pair + 1, ((early, 0), (early, 2)), 2)
        if r == 2 and n % NH != NH - 2:
            put("V", pair + 1, ((early, 4), (early, 6), (late, 7)))
        if r == 3 and n % NH != NH - 1:
            put("V", pair + 1, ((early, 6),), 3)
        if r == 3:
            put("Q", quad + 1, ((early, 1), (late, 1), (early, 2), (late, 2), (early, 3), (late, 3), (early, 4), (early, 5)))
        if n % NH == NH - 1:
            put("V", pair + 1, ((late, 4), (late, 5), (late, 6), (early, 7)))
    order, bank = list(before), {}
    for j, piece in enumerate(before):
        bank[piece] = ("m", 0, 1)[j % 3]
    for g in range(LAST + 1):
        order += early[g] + late[g]
        for piece in early[g] + late[g]:
            bank[piece] = g % 2 if piece in early[g] and g < NG and g % NI < 4 else "m"
    return before, early, late, order, bank


def plan_splits():
    before = [("Wk", 0), ("Wv", 0), ("Wk", 1)]
    at = {}
    for n in range(NHD):
        r = n % 4
        if n + 2 < NHD:
            at.setdefault((n, 1), []).append(("Wk", n + 2))
        if r == 0:
            at.setdefault((n, 2), []).append(("Wv", n // 2 + 1))
        if r == 1 and n // 2 + 2 < NHD // 2:
            at.setdefault((n, 6), []).append(("Wv", n // 2 + 2))
        if r % 2 == 0:
            at.setdefault((n, 6), []).append(("Wo", n // 2))
    order = list(before)
    for key in sorted(at):
        order += at[key]
    return before, at, {s: j for j, s in enumerate(order)}


def attention_ffn_block(nc, x, Wq, bq, Wk, bk, Wv, bv, Wo, bo, w_gate, w_up, w_down, out):
    before, early, late, pieces, bank_of = plan_pieces()
    piece_no = {piece: j for j, piece in enumerate(pieces)}
    out_count, before_in_bank, made, latest = {}, {}, {"Q": 0, "other": 0}, {}
    for piece in pieces:
        kind = "Q" if piece[0] == "Q" else "other"
        made[kind] += 1
        out_count[piece] = made[kind]
        before_in_bank[piece] = latest.get(bank_of[piece])
        latest[bank_of[piece]] = piece
    splits_before, splits_at, split_no = plan_splits()
    hi_count, c = {}, 0
    for piece in pieces:
        c += piece[0] in "KV"
        hi_count[piece] = c

    xnT_dram = nc.dram_tensor("xnT_dram", [B, 2, P, KT, T], F32, kind="Internal").ap()
    base_dram = nc.dram_tensor("base_dram", [B * T, D], F32, kind="Internal").ap()

    x_rows = x.rearrange("b t d -> (b t) d").rearrange("(n p) d -> p n d", p=P)
    base_rows = base_dram.rearrange("(n p) d -> p n d", p=P)
    out_rows = out.rearrange("b t d -> (b t) d").rearrange("(n p) d -> p n d", p=P)
    Wq_rows = Wq.rearrange("(k p) n -> p k n", p=P)
    Wk_rows = Wk.rearrange("(k p) n -> p k n", p=P)
    Wv_rows = Wv.rearrange("(k p) n -> p k n", p=P)
    Wo_rows = Wo.rearrange("(h p) n -> p h n", p=P)

    ctx = ExitStack()
    with ctx:
        def sb(name, shape, dt, where=ctx):
            return where.enter_context(nc.sbuf_tensor(name, shape, dt))

        def sb2(name, shape, where=ctx):
            return [sb(f"{name}_{part}", shape, F32R, where) for part in ("hi", "lo")]

        def sem(name):
            return ctx.enter_context(nc.semaphore(name))

        ident = sb("ident", [P, P], F32)
        mask = sb("mask", [P, P], F32)
        bias_rows = sb("bias_rows", [3 * NH, P], F32)
        bias = sb("bias", [P, 3 * NH], F32)
        bqs_sb = sb("bqs_sb", [P, RQ], F32)
        bq_sb, bk_sb, bv_sb = (bias[:, j * NH:(j + 1) * NH] for j in range(3))

        a = ExitStack()
        raw_w = sb("raw_w", [P, 3 * KT * HID], F32, a)
        sil = sb("sil", [P, 2, CH], F32, a)
        y_stage = sb("y_stage", [P, 2, 2, D], F32, a)
        wgT = sb2("wgT", [P, KT, HID], a)
        wuT = sb2("wuT", [P, KT, HID], a)
        xnT_a = sb2("xnT_a", [P, 2, KT, CH], a)
        wdT = sb2("wdT", [P, HT, D], a)
        x_sb = sb("x_sb", [P, NT, D], F32, a)
        hid = sb2("hid", [P, 2, HT, CH], a)
        xn_sb = sb("xn_sb", [P, CT, D], F32, a)
        bo_sb = sb("bo_sb", [P, D], F32, a)
        stats = sb("stats", [P, 2, 6], F32, a)
        mean_var = sb("mean_var", [P, NT, 2], F32, a)
        var_eps = sb("var_eps", [P, NT], F32, a)
        std = sb("std", [P, NT], F32, a)
        rstd = sb("rstd", [P, NT], F32, a)
        newton = sb("newton", [P, NT], F32, a)
        a.close()
        wg_raw = raw_w[:, 0:KT * HID].rearrange("p (n d) -> p n d", d=D)
        wu_raw = raw_w[:, KT * HID:2 * KT * HID].rearrange("p (n d) -> p n d", d=D)
        wd_raw = raw_w[:, 2 * KT * HID:3 * KT * HID].rearrange("p (n h) -> p n h", h=HID)
        wq_raw = raw_w[:, 0:KT * HD].rearrange("p (k n) -> p k n", k=KT)

        v = sb2("v", [P, 2, NI, 2 * DH])
        wq = sb2("wq", [P, KT, HD])
        xnT = sb2("xnT", [P, KT, T])
        qT = sb("qT", [P, GROUP, T], F32)
        q = sb2("q", [P, 2, BANK])
        k = sb2("k", [P, 2, T])
        prob = sb("prob", [P, 3, T], F32)
        pT = [sb2("pT_even", [P, NI - 2, QC]), sb2("pT_odd", [P, NI, QC])]
        oT_even = sb2("oT_even", [P, T])
        oT_odd = sb2("oT_odd", [P, 2, QC])
        y = sb("y", [P, NI, D], F32)
        wk_raw = sb("wk_raw", [P, 2, KT, DH], F32)
        wk = sb2("wk", [P, 2, KT, DH])
        wv_raw = sb("wv_raw", [P, KT, 2 * DH], F32)
        wv = sb2("wv", [P, KT, 2 * DH])
        wo_raw = sb("wo_raw", [P, 2, D], F32)
        wo = sb2("wo", [P, 2, D])
        neg_max = sb("neg_max", [P, 4], F32)
        row_sum = sb("row_sum", [P, 4], F32)
        inv_sum = sb("inv_sum", [P, 4], F32)

        def pb(name, cols):
            return ctx.enter_context(nc.psum_tensor(name, [P, cols], F32))

        s_ps = [pb("s_ps0", 2 * BANK), pb("s_ps1", 2 * BANK)]
        t_ps = [pb("t_ps0", BANK), pb("t_ps1", BANK)]
        o_ps = pb("o_ps", BANK)
        m_ps = pb("m_ps", BANK)

        s_x = [sem(f"s_x{n}") for n in range(NC)]
        s_wg, s_wu, s_wd, s_wqraw = sem("s_wg"), sem("s_wu"), sem("s_wd"), sem("s_wqraw")
        s_bias, s_bo = sem("s_bias"), sem("s_bo")
        s_xst = [sem("s_xst0"), sem("s_xst1")]
        s_yst = [sem("s_yst0"), sem("s_yst1")]
        s_xload = [sem("s_xload_hi"), sem("s_xload_lo")]
        s_wkraw = [sem("s_wkraw0"), sem("s_wkraw1")]
        s_wvraw, s_woraw = sem("s_wvraw"), sem("s_woraw")
        s_base = [sem(f"s_base{j}") for j in range(NK)]
        s_out = [sem(f"s_out{j}") for j in range(NK)]
        s_const, s_biasT, s_bcol, s_bqs = sem("s_const"), sem("s_biasT"), sem("s_bcol"), sem("s_bqs")
        s_stat = sem("s_stat")
        s_veps = sem("s_veps")
        s_std = sem("s_std")
        s_xn = sem("s_xn")
        s_ta = sem("s_ta")
        s_tahi = sem("s_tahi")
        s_talo = sem("s_talo")
        s_gate, s_up = sem("s_gate"), sem("s_up")
        s_silu, s_h = sem("s_silu"), sem("s_h")
        s_hidhi, s_hid = sem("s_hidhi"), sem("s_hid")
        s_xbo = sem("s_xbo")
        s_down = sem("s_down")
        s_ffn = sem("s_ffn")
        s_wqhi, s_wq = sem("s_wqhi"), sem("s_wq")
        s_qk = sem("s_qk")
        s_masked = sem("s_masked")
        s_max = sem("s_max")
        s_exp = sem("s_exp")
        s_inv = sem("s_inv")
        s_norm = sem("s_norm")
        s_t = sem("s_t")
        s_thi, s_tlo = sem("s_thi"), sem("s_tlo")
        s_pv = sem("s_pv")
        s_ohi, s_olo = sem("s_ohi"), sem("s_olo")
        s_fill = sem("s_fill")
        s_fillhi = sem("s_fillhi")
        s_qout, s_pout = sem("s_qout"), sem("s_pout")
        s_qhi, s_q = sem("s_qhi"), sem("s_q")
        s_splithi, s_split = sem("s_splithi"), sem("s_split")

        def waits(eng):
            seen = {}

            def need(s, count):
                if count > seen.get(id(s), 0):
                    seen[id(s)] = count
                    eng.wait_ge(s, count)
            return need

        def need_out(need, piece):
            need(s_qout if piece[0] == "Q" else s_pout, out_count[piece])

        def piece_ps(piece):
            where = bank_of[piece]
            return m_ps[:, :] if where == "m" else s_ps[where][:, BANK:2 * BANK]

        a_banks = [("wg", j) for j in range(4)] + [("x", 0, kt) for kt in range(KT)]
        a_banks += [("wu", j) for j in range(4)] + [("wd", j) for j in range(4)]
        a_banks += [("x", c, kt) for c in range(1, NC) for kt in range(KT)]
        a_bank_no = {b: j for j, b in enumerate(a_banks)}

        def a_dst(b, part):
            if b[0] == "x":
                return xnT_a[part][:, b[1] % 2, b[2], :]
            if b[0] == "wd":
                return wdT[part][:, 2 * b[1]:2 * b[1] + 2, :].rearrange("p n d -> p (n d)")
            kt, half = divmod(b[1], 2)
            return (wgT if b[0] == "wg" else wuT)[part][:, kt, half * BANK:(half + 1) * BANK]

        def o_slot(n, kc):
            if n % 2 == 0:
                return ([t[:, kc * QC:(kc + 1) * QC] for t in oT_even], ("y", n // 2 - 1, kc) if n >= 2 else None)
            j = (n // 2) * NK + kc - 2
            return ([t[:, kc % 2, :] for t in oT_odd], ("y", j // NK, j % NK) if j >= 0 else None)

        std_groups = [(0, 1), (1, 2), (2, NC)]

        block = ctx.enter_context(nc.Block())

        @block.sync
        def _(eng):
            need = waits(eng)

            def load_x(c):
                eng.dma_start(x_sb[:, c * CT:(c + 1) * CT, :], x_rows[:, c * CT:(c + 1) * CT, :]).then_inc(s_x[c], 16)

            load_x(0)
            eng.dma_start(wg_raw, w_gate.rearrange("(n p) d -> p n d", p=P)).then_inc(s_wg, 16)
            eng.dma_start(wu_raw, w_up.rearrange("(n p) d -> p n d", p=P)).then_inc(s_wu, 16)
            load_x(1)
            eng.dma_start(wd_raw, w_down.rearrange("(n p) h -> p n h", p=P)).then_inc(s_wd, 16)
            eng.dma_start(bo_sb[:, :], bo.partition_broadcast(P)).then_inc(s_bo, 16)
            for c in range(2, NC):
                load_x(c)
            for j, src in enumerate((bq, bk, bv)):
                eng.dma_start(bias_rows[j * NH:(j + 1) * NH, :], src.rearrange("(h p) -> h p", p=P)).then_inc(s_bias, 16)

            def store_xnT(c):
                need(s_talo, a_bank_no[("x", c, KT - 1)] + 1)
                b, half = divmod(c, T // CH)
                for part in range(2):
                    eng.dma_start(xnT_dram[b, part][:, :, half * CH:(half + 1) * CH],
                                  xnT_a[part][:, c % 2, :, :].bitcast(F32)).then_inc(s_xst[c % 2], 16)

            def store_base(c):
                for d in range(2):
                    need(s_ffn, 2 * c + d + 1)
                    t0 = c * CT + 2 * d
                    eng.dma_start(base_rows[:, t0:t0 + 2, :], y_stage[:, d, :, :]).then_inc(s_yst[d], 16)

            store_xnT(0)
            for c in range(NC):
                if c + 1 < NC:
                    store_xnT(c + 1)
                if c == 0:
                    need(s_ta, a_bank_no[("wd", 3)] + 1)
                    eng.dma_start(wq_raw, Wq_rows).then_inc(s_wqraw, 16)
                if c >= 1:
                    store_base(c - 1)

            def load_xnT(b):
                for part in range(2):
                    eng.dma_start(xnT[part][:, :, :].bitcast(F32), xnT_dram[b, part]).then_inc(s_xload[part], 16)

            need(s_up, NC * HT)
            for slot in range(2):
                need(s_xst[slot], 32 * (NC // 2))
            load_xnT(0)
            store_base(NC - 1)
            need(s_down, 2 * NC)
            need(s_ffn, 2 * NC)

            def load_wk(n):
                h = n % NH
                if n >= 2:
                    need(s_split, split_no[("Wk", n - 2)] + 1)
                eng.dma_start(wk_raw[:, n % 2, :, :], Wk_rows[:, :, h * DH:(h + 1) * DH]).then_inc(s_wkraw[n % 2], 16)

            def load_wv(pair):
                h = 2 * pair % NH
                if pair >= 1:
                    need(s_split, split_no[("Wv", pair - 1)] + 1)
                eng.dma_start(wv_raw[:, :, :], Wv_rows[:, :, h * DH:(h + 2) * DH]).then_inc(s_wvraw, 16)

            def load_wo(pair):
                h = 2 * pair % NH
                if pair >= 1:
                    need(s_split, split_no[("Wo", pair - 1)] + 1)
                eng.dma_start(wo_raw[:, :, :], Wo_rows[:, h:h + 2, :]).then_inc(s_woraw, 16)

            def load_base(b, j):
                if b >= 1:
                    need(s_out[j], 16 * b)
                t0 = b * NI + 2 * j
                eng.dma_start(y[:, 2 * j:2 * j + 2, :], base_rows[:, t0:t0 + 2, :]).then_inc(s_base[j], 16)

            def store_out(b, j):
                need_out(need, ("y", (b + 1) * NH // 2 - 1, j))
                t0 = b * NI + 2 * j
                eng.dma_start(out_rows[:, t0:t0 + 2, :], y[:, 2 * j:2 * j + 2, :]).then_inc(s_out[j], 16)

            load_wk(0)
            load_wv(0)
            load_wk(1)
            load_wo(0)
            for slot in range(2):
                need(s_yst[slot], 16 * NC)
            for j in range(NK):
                load_base(0, j)
            for n in range(NHD):
                r, b = n % 4, n // NH
                if n + 2 < NHD:
                    load_wk(n + 2)
                if r == 0:
                    load_wv(n // 2 + 1)
                if r == 1 and n // 2 + 2 < NHD // 2:
                    load_wv(n // 2 + 2)
                if r % 2 == 0 and n:
                    load_wo(n // 2)
                if n % NH == 0 and n:
                    for j in range(NK):
                        store_out(b - 1, j)
                        load_base(b, j)
                if n % NH == NH - 2 and b + 1 < B:
                    need(s_fill, piece_no[("K", n + 1, 1)] + 1)
                    load_xnT(b + 1)
            for j in range(NK):
                store_out(B - 1, j)
            for j in range(NK):
                need(s_out[j], 16 * B)

        @block.gpsimd
        def _(eng):
            need = waits(eng)
            eng.memset(ident[:, :], 0.0).then_inc(s_const, 1)
            eng.memset(mask[:, :], 0.0).then_inc(s_const, 1)
            need(s_const, 2)
            eng.affine_select(out=ident[:, :], in_=ident[:, :], compare_op=ALU.not_equal, fill=1.0,
                              base=0, pattern=[[-1, P]], channel_multiplier=1).then_inc(s_const, 1)
            eng.affine_select(out=mask[:, :], in_=mask[:, :], compare_op=ALU.is_ge, fill=MASKED,
                              base=0, pattern=[[-1, P]], channel_multiplier=1).then_inc(s_const, 1)

            count = {}

            def split(dst, src, sem_hi, sem_lo, index):
                count[id(sem_hi)] = count.get(id(sem_hi), 0) + 1
                eng.tensor_scalar(index(dst[0]), src, 1.0, 1.0, ALU.mult, ALU.mult).then_inc(sem_hi, 1)
                need(sem_hi, count[id(sem_hi)])
                eng.tensor_tensor(index(dst[1]), src, index(dst[0]), ALU.subtract).then_inc(sem_lo, 1)

            for c in range(NC):
                for ht in range(HT):
                    u = c * HT + ht
                    if ht == 0:
                        need(s_xn, c + 1)
                        need(s_bo, 16)
                        for t in range(c * CT, (c + 1) * CT):
                            ins = eng.tensor_tensor(x_sb[:, t, :], x_sb[:, t, :], bo_sb[:, :], ALU.add)
                        ins.then_inc(s_xbo, 1)
                        if c >= 2:
                            need(s_down, 2 * (c - 1))
                    need(s_h, u + 1)
                    split(hid, sil[:, u % 2, :], s_hidhi, s_hid, lambda t: t[:, c % 2, ht, :])

            need(s_wqraw, 16)
            need(s_up, NC * HT)
            for kt in range(KT):
                for half in range(2):
                    cols = slice(half * HD // 2, (half + 1) * HD // 2)
                    split(wq, wq_raw[:, kt, cols], s_wqhi, s_wq, lambda t: t[:, kt, cols])
            need(s_down, 2 * NC)
            need(s_ffn, 2 * NC)

            def split_weight(which):
                what, j = which
                if what == "Wk":
                    need(s_wkraw[j % 2], 16 * (j // 2 + 1))
                    if j >= 2:
                        need(s_fill, piece_no[("K", j - 2, 1)] + 1)
                    split(wk, wk_raw[:, j % 2, :, :], s_splithi, s_split, lambda t: t[:, j % 2, :, :])
                elif what == "Wv":
                    need(s_wvraw, 16 * (j + 1))
                    if j:
                        need(s_fill, piece_no[("V", j - 1, 3)] + 1)
                    split(wv, wv_raw[:, :, :], s_splithi, s_split, lambda t: t[:, :, :])
                else:
                    need(s_woraw, 16 * (j + 1))
                    if j:
                        need(s_fill, piece_no[("y", j - 1, NK - 1)] + 1)
                    split(wo, wo_raw[:, :, :], s_splithi, s_split, lambda t: t[:, :, :])

            def split_q(n, half):
                need_out(need, ("Q", n // GROUP, 7))
                if n:
                    need(s_qk, NI * (n - 1) + 4 * (half + 1))
                split(q, qT[:, n % GROUP, half * BANK:(half + 1) * BANK], s_qhi, s_q, lambda t: t[:, half, :])

            for which in splits_before:
                split_weight(which)
            split_q(0, 0)
            for g in range(NG + 1):
                if g >= 1:
                    j, L = g - 1, ((g - 1) % NI + 1) * P
                    need(s_inv, j + 1)
                    eng.tensor_scalar(prob[:, j % 3, 0:L], prob[:, j % 3, 0:L], inv_sum[:, j % 4:j % 4 + 1], 1.0,
                                      ALU.mult, ALU.mult).then_inc(s_norm, 1)
                if g == NG:
                    break
                n, i = divmod(g, NI)
                if i == 0:
                    split_q(n, 1)
                for which in splits_at.get((n, i), []):
                    split_weight(which)
                if i == (6 if n % GROUP == GROUP - 1 else 5) and n + 1 < NHD:
                    split_q(n + 1, 0)

        @block.scalar
        def _(eng):
            need = waits(eng)

            def roots(j):
                t0, t1 = std_groups[j][0] * CT, std_groups[j][1] * CT
                need(s_veps, j + 1)
                eng.activation(std[:, t0:t1], var_eps[:, t0:t1], ACT.Sqrt).then_inc(s_std, 1)

            def part_hi(b):
                j = a_bank_no[b]
                need(s_ta, j + 1)
                if b[0] == "x" and b[1] >= 2:
                    need(s_up, (b[1] - 1) * HT)
                    need(s_xst[b[1] % 2], 32 * (b[1] // 2))
                eng.activation(a_dst(b, 0), t_ps[j % 2][:, :], ACT.Copy).then_inc(s_tahi, 1)

            roots(0)
            for b in a_banks[:10]:
                part_hi(b)
            for c in range(NC):
                for ht in range(HT):
                    u = c * HT + ht
                    need(s_gate, u + 1)
                    if u >= 2:
                        need(s_hid, u - 1)
                    eng.activation(sil[:, u % 2, :], s_ps[u % 2][:, 0:CH], ACT.Silu).then_inc(s_silu, 1)
                    if ht == 1 and c + 1 < len(std_groups):
                        roots(c + 1)
                    if ht == 3:
                        if c == 0:
                            for b in a_banks[10:14]:
                                part_hi(b)
                        if c + 1 < NC:
                            for kt in range(KT):
                                part_hi(("x", c + 1, kt))

            need(s_biasT, 1)
            eng.activation(bias[:, :], t_ps[0][:, 0:3 * NH], ACT.Copy).then_inc(s_bcol, 1)
            need(s_bcol, 1)
            eng.activation(bqs_sb[:, :], bq_sb, ACT.Copy, scale=SCALE).then_inc(s_bqs, 1)
            need(s_bqs, 1)
            need(s_ffn, 2 * NC)
            need(s_hid, NC * HT)
            for slot in range(2):
                need(s_yst[slot], 16 * NC)

            def piece_out(piece):
                what, j, m = piece
                ps = piece_ps(piece)
                if what == "y":
                    return
                need(s_fill, piece_no[piece] + 1)
                if what == "K":
                    if j >= 2:
                        need(s_qk, NI * (j - 1))
                    h = j % NH
                    eng.activation(k[0][:, j % 2, m * BANK:(m + 1) * BANK], ps, ACT.Identity,
                                   bias=bk_sb[:, h:h + 1]).then_inc(s_fillhi, 1)
                elif what == "V":
                    need(s_wq, 4)
                    if j >= 2:
                        need(s_pv, NK * 2 * (j - 1))
                    eng.activation(v[0][:, j % 2, 2 * m:2 * m + 2, :].rearrange("p n d -> p (n d)"), ps,
                                   ACT.Copy).then_inc(s_fillhi, 1)
                else:
                    if j:
                        need(s_q, 2 * GROUP * j)
                    for c2 in range(2):
                        c = 2 * m + c2
                        dst = qT[:, :, :].rearrange("p h (r c) -> p c h r", c=RQ)[:, c]
                        src = ps[:, c2 * QC:(c2 + 1) * QC].rearrange("p (h r) -> p h r", h=GROUP)
                        ins = eng.activation(dst, src, ACT.Identity, bias=bqs_sb[:, c:c + 1], scale=SCALE)
                    ins.then_inc(s_qout, 1)

            for piece in before:
                piece_out(piece)
            for g in range(LAST + 1):
                j = g - 1
                if 0 <= j < NG:
                    L = (j % NI + 1) * P
                    need(s_max, j + 1)
                    if j >= 3:
                        need(s_t, t_banks_through(j - 3))
                    c0, c1 = score_cols(j % NI)
                    eng.activation(prob[:, j % 3, 0:L], s_ps[j % 2][:, c0:c1], ACT.Exp,
                                   bias=neg_max[:, j % 4:j % 4 + 1],
                                   accum_out=row_sum[:, j % 4:j % 4 + 1]).then_inc(s_exp, 1)
                for piece in early[g]:
                    piece_out(piece)
                j = g - PV_LAG
                if 0 <= j < NG and j % 2 == 1:
                    n, kc = j // NI, (j % NI) // 2
                    ck = n * NK + kc
                    need(s_pv, ck + 1)
                    dst, last_read = o_slot(n, kc)
                    if last_read:
                        need(s_fill, piece_no[last_read] + 1)
                    h = n % NH
                    eng.activation(dst[0], o_ps[:, 0:QC], ACT.Identity, bias=bv_sb[:, h:h + 1]).then_inc(s_ohi, 1)
                for piece in late[g]:
                    piece_out(piece)
                j = g - T_LAG
                if 0 <= j < NG:
                    n, i = divmod(j, NI)
                    kc = i // 2
                    ck = n * NK + kc
                    if ck >= 2:
                        need(s_pv, ck - 1)
                    for bank in range((i + 4) // 4):
                        tb = t_banks_through(j - 1) + bank
                        k0, k1 = 4 * bank, min(4 * bank + 4, i + 1)
                        need(s_t, tb + 1)
                        eng.activation(pT[kc % 2][0][:, k0:k1, (i % 2) * P:(i % 2 + 1) * P],
                                       t_ps[tb % 2][:, 0:(k1 - k0) * P].rearrange("p (n t) -> p n t", t=P),
                                       ACT.Copy).then_inc(s_thi, 1)

        @block.vector
        def _(eng):
            need = waits(eng)
            chain = [0]

            def link(ins):
                chain[0] += 1
                ins.then_inc(s_stat, 1)
                need(s_stat, chain[0])

            def statistics(c):
                need(s_x[c], 16)
                for t in range(c * CT, (c + 1) * CT):
                    link(eng.bn_stats(stats[:, t % 2, :], x_sb[:, t, :]))
                    link(eng.bn_aggr(mean_var[:, t, :], stats[:, t % 2, :]))

            def plus_eps(j):
                t0, t1 = std_groups[j][0] * CT, std_groups[j][1] * CT
                eng.tensor_scalar(var_eps[:, t0:t1], mean_var[:, t0:t1, 1], EPS, None, ALU.add).then_inc(s_veps, 1)

            def inverse_std(j):
                t0, t1 = std_groups[j][0] * CT, std_groups[j][1] * CT
                r, w, s = rstd[:, t0:t1], newton[:, t0:t1], var_eps[:, t0:t1]
                need(s_veps, j + 1)
                need(s_std, j + 1)
                link(eng.reciprocal(r, std[:, t0:t1]))
                link(eng.tensor_tensor(w, r, r, ALU.mult))
                link(eng.tensor_tensor(w, w, s, ALU.mult))
                link(eng.tensor_scalar(w, w, -0.5, 1.5, ALU.mult, ALU.add))
                link(eng.tensor_tensor(r, r, w, ALU.mult))

            def normed(c):
                if c:
                    need(s_ta, a_bank_no[("x", c - 1, KT - 1)] + 1)
                for j in range(CT):
                    t = c * CT + j
                    ins = eng.tensor_scalar(xn_sb[:, j, :], x_sb[:, t, :], mean_var[:, t, 0:1], rstd[:, t:t + 1],
                                            ALU.subtract, ALU.mult)
                ins.then_inc(s_xn, 1)

            def part_lo(b):
                j = a_bank_no[b]
                need(s_tahi, j + 1)
                eng.tensor_tensor(a_dst(b, 1), t_ps[j % 2][:, :], a_dst(b, 0), ALU.subtract).then_inc(s_talo, 1)

            def base_out(c):
                need(s_xbo, c + 1)
                for d in range(2):
                    need(s_down, 2 * c + d + 1)
                    if c:
                        need(s_yst[d], 16 * c)
                    t0 = c * CT + 2 * d
                    eng.tensor_tensor(y_stage[:, d, :, :].rearrange("p n d -> p (n d)"), (o_ps, m_ps)[d][:, :],
                                      x_sb[:, t0:t0 + 2, :].rearrange("p n d -> p (n d)"), ALU.add).then_inc(s_ffn, 1)

            statistics(0)
            plus_eps(0)
            inverse_std(0)
            normed(0)
            for b in a_banks[:10]:
                part_lo(b)
            for c in range(NC):
                for ht in range(HT):
                    u = c * HT + ht
                    if c == 0 and ht == 1:
                        statistics(1)
                        plus_eps(1)
                    if c == 0 and ht >= 3:
                        statistics(ht - 1)
                    if c == 1 and ht == 0:
                        statistics(NC - 1)
                        plus_eps(2)
                    need(s_up, u + 1)
                    need(s_silu, u + 1)
                    eng.tensor_tensor(sil[:, u % 2, :], sil[:, u % 2, :], s_ps[u % 2][:, CH:2 * CH], ALU.mult)\
                       .then_inc(s_h, 1)
                    if ht == 1 and c + 1 < len(std_groups):
                        inverse_std(c + 1)
                    if ht == 2 and c + 1 < NC:
                        normed(c + 1)
                    if ht == 3:
                        if c == 0:
                            for b in a_banks[10:14]:
                                part_lo(b)
                        if c + 1 < NC:
                            for kt in range(KT):
                                part_lo(("x", c + 1, kt))
                if c >= 1:
                    base_out(c - 1)
            base_out(NC - 1)

            need(s_bcol, 1)
            need(s_const, 4)
            need(s_hid, NC * HT)
            for slot in range(2):
                need(s_yst[slot], 16 * NC)

            def piece_out(piece):
                what, j, m = piece
                ps = piece_ps(piece)
                if what == "Q":
                    return
                if what == "y":
                    b, pair = divmod(j, NH // 2)
                    need(s_fill, piece_no[piece] + 1)
                    need(s_base[m], 16 * (b + 1))
                    if pair:
                        need_out(need, ("y", j - 1, m))
                    rows = y[:, 2 * m:2 * m + 2, :].rearrange("p n d -> p (n d)")
                    eng.tensor_tensor(rows, ps, rows, ALU.add).then_inc(s_pout, 1)
                    return
                need(s_fillhi, hi_count[piece])
                if what == "K":
                    h, cols = j % NH, slice(m * BANK, (m + 1) * BANK)
                    eng.scalar_tensor_tensor(out=k[1][:, j % 2, cols], in0=ps, scalar=bk_sb[:, h:h + 1],
                                             in1=k[0][:, j % 2, cols], op0=ALU.add, op1=ALU.subtract)\
                       .then_inc(s_pout, 1)
                else:
                    hi, lo = (t[:, j % 2, 2 * m:2 * m + 2, :].rearrange("p n d -> p (n d)") for t in v)
                    eng.tensor_tensor(lo, ps, hi, ALU.subtract).then_inc(s_pout, 1)

            for piece in before:
                piece_out(piece)
            for g in range(LAST + 1):
                if g < NG:
                    need(s_qk, g + 1)
                    if g >= 4:
                        need(s_exp, g - 3)
                    c0, c1 = score_cols(g % NI)
                    diagonal = s_ps[g % 2][:, c1 - P:c1]
                    eng.tensor_tensor(diagonal, diagonal, mask[:, :], ALU.add).then_inc(s_masked, 1)
                    need(s_masked, g + 1)
                    eng.tensor_reduce(neg_max[:, g % 4:g % 4 + 1], s_ps[g % 2][:, c0:c1], AX_X, ALU.max,
                                      negate=True).then_inc(s_max, 1)
                for piece in early[g]:
                    piece_out(piece)
                if 1 <= g <= NG:
                    j = g - 1
                    need(s_exp, j + 1)
                    if j >= 4:
                        need(s_norm, j - 3)
                    eng.reciprocal(inv_sum[:, j % 4:j % 4 + 1], row_sum[:, j % 4:j % 4 + 1]).then_inc(s_inv, 1)
                j = g - PV_LAG
                if 0 <= j < NG and j % 2 == 1:
                    n, kc = j // NI, (j % NI) // 2
                    need(s_ohi, n * NK + kc + 1)
                    dst, _ = o_slot(n, kc)
                    h = n % NH
                    eng.scalar_tensor_tensor(out=dst[1], in0=o_ps[:, 0:QC], scalar=bv_sb[:, h:h + 1], in1=dst[0],
                                             op0=ALU.add, op1=ALU.subtract).then_inc(s_olo, 1)
                for piece in late[g]:
                    piece_out(piece)
                j = g - T_LAG
                if 0 <= j < NG:
                    n, i = divmod(j, NI)
                    kc = i // 2
                    for bank in range((i + 4) // 4):
                        tb = t_banks_through(j - 1) + bank
                        k0, k1 = 4 * bank, min(4 * bank + 4, i + 1)
                        need(s_thi, tb + 1)
                        hi, lo = (t[:, k0:k1, (i % 2) * P:(i % 2 + 1) * P] for t in pT[kc % 2])
                        eng.tensor_tensor(lo, t_ps[tb % 2][:, 0:(k1 - k0) * P].rearrange("p (n t) -> p n t", t=P), hi,
                                          ALU.subtract).then_inc(s_tlo, 1)

        @block.tensor
        def _(eng):
            need = waits(eng)

            def product(dst, terms):
                for j, (sta, mov) in enumerate(terms):
                    for s, m in HILO:
                        ins = eng.matmul(dst, sta[s], mov[m], start=(j == 0 and (s, m) == HILO[0]),
                                         stop=(j == len(terms) - 1 and (s, m) == HILO[-1]))
                return ins

            def parts(t, index):
                return [index(t[0]), index(t[1])]

            def transposes(b):
                j = a_bank_no[b]
                need(s_const, 3)
                if b[0] == "x":
                    need(s_xn, b[1] + 1)
                    src = [xn_sb[:, t, b[2] * P:(b[2] + 1) * P] for t in range(CT)]
                elif b[0] == "wd":
                    need(s_wd, 16)
                    src = [wd_raw[:, dt, ht * P:(ht + 1) * P] for ht in (2 * b[1], 2 * b[1] + 1) for dt in range(KT)]
                else:
                    need(s_wg if b[0] == "wg" else s_wu, 16)
                    kt, half = divmod(b[1], 2)
                    raw = wg_raw if b[0] == "wg" else wu_raw
                    src = [raw[:, 4 * half + ht, kt * P:(kt + 1) * P] for ht in range(4)]
                if j >= 2:
                    need(s_talo, j - 1)
                for c, s in enumerate(src):
                    ins = eng.transpose(t_ps[j % 2][:, c * P:(c + 1) * P], s, ident[:, :])
                ins.then_inc(s_ta, 1)

            def gate_up(c, ht):
                u = c * HT + ht
                need(s_talo, a_bank_no[("x", c, KT - 1)] + 1)
                if u == 0:
                    need(s_talo, a_bank_no[("wu", 3)] + 1)
                if u >= 2:
                    need(s_h, u - 1)
                for w, half, done in ((wgT, 0, s_gate), (wuT, 1, s_up)):
                    terms = [(parts(w, lambda t: t[:, kt, ht * P:(ht + 1) * P]),
                              parts(xnT_a, lambda t: t[:, c % 2, kt, :])) for kt in range(KT)]
                    product(s_ps[u % 2][:, half * CH:(half + 1) * CH], terms).then_inc(done, 1)

            def down(c):
                need(s_talo, a_bank_no[("wd", 3)] + 1)
                need(s_hid, (c + 1) * HT)
                for d in range(2):
                    if c:
                        need(s_ffn, 2 * (c - 1) + d + 1)
                    for t2 in range(2):
                        t = 2 * d + t2
                        terms = [(parts(hid, lambda h: h[:, c % 2, ht, t * P:(t + 1) * P]),
                                  parts(wdT, lambda w: w[:, ht, :])) for ht in range(HT)]
                        ins = product((o_ps, m_ps)[d][:, t2 * D:(t2 + 1) * D], terms)
                    ins.then_inc(s_down, 1)

            for b in a_banks[:10]:
                transposes(b)
            for c in range(NC):
                for ht in range(HT):
                    gate_up(c, ht)
                    if ht == 3:
                        if c == 0:
                            for b in a_banks[10:14]:
                                transposes(b)
                        if c + 1 < NC:
                            for kt in range(KT):
                                transposes(("x", c + 1, kt))
                if c >= 1:
                    down(c - 1)
            down(NC - 1)

            need(s_bias, 48)
            need(s_talo, len(a_banks))
            eng.transpose(t_ps[0][:, 0:3 * NH], bias_rows[:, :], ident[0:3 * NH, 0:3 * NH]).then_inc(s_biasT, 1)
            need(s_ffn, 2 * NC)

            def issue_piece(piece):
                what, j, m = piece
                ps = piece_ps(piece)
                if before_in_bank[piece]:
                    need_out(need, before_in_bank[piece])
                if what == "y":
                    need(s_split, split_no[("Wo", j)] + 1)
                    need(s_olo, NK * (2 * j + 1) + m + 1)
                    for t2 in range(2):
                        even = parts(oT_even, lambda t: t[:, (2 * m + t2) * P:(2 * m + t2 + 1) * P])
                        odd = parts(oT_odd, lambda t: t[:, m % 2, t2 * P:(t2 + 1) * P])
                        terms = [(o, parts(wo, lambda t: t[:, hh, :])) for hh, o in enumerate((even, odd))]
                        ins = product(ps[:, t2 * D:(t2 + 1) * D], terms)
                    ins.then_inc(s_fill, 1)
                    return
                heads_per = {"K": 1, "V": 2, "Q": GROUP}[what]
                for part in range(2):
                    need(s_xload[part], 16 * (j * heads_per // NH + 1))
                if what == "K":
                    need(s_split, split_no[("Wk", j)] + 1)
                    terms = [(parts(wk, lambda t: t[:, j % 2, kt, :]),
                              parts(xnT, lambda t: t[:, kt, m * BANK:(m + 1) * BANK])) for kt in range(KT)]
                    ins = product(ps, terms)
                elif what == "V":
                    need(s_split, split_no[("Wv", j)] + 1)
                    for t2 in range(2):
                        st = 2 * m + t2
                        terms = [(parts(xnT, lambda t: t[:, kt, st * P:(st + 1) * P]),
                                  parts(wv, lambda t: t[:, kt, :])) for kt in range(KT)]
                        ins = product(ps[:, t2 * 2 * DH:(t2 + 1) * 2 * DH], terms)
                else:
                    need(s_wq, 4)
                    tok = j * GROUP % NH * QTOK
                    for c2 in range(2):
                        c = 2 * m + c2
                        terms = [(parts(wq, lambda t: t[:, kt, c * P:(c + 1) * P]),
                                  parts(xnT, lambda t: t[:, kt, tok:tok + QC])) for kt in range(KT)]
                        ins = product(ps[:, c2 * QC:(c2 + 1) * QC], terms)
                ins.then_inc(s_fill, 1)

            def scores(g):
                n, i = divmod(g, NI)
                need_out(need, ("K", n, 1))
                need(s_q, 2 * n + i // 4 + 1)
                if g >= 2:
                    need(s_exp, g - 1)
                if i in (4, 5):
                    for piece in [p for s in range(i - 4, 4, 2) for p in early[n * NI + s]]:
                        need_out(need, piece)
                c0, c1 = score_cols(i)
                qi = parts(q, lambda t: t[:, i // 4, (i % 4) * P:(i % 4 + 1) * P])
                for p0, p1 in ((c0, min(c1, BANK)), (BANK, c1)):
                    if p0 < p1:
                        ki = parts(k, lambda t: t[:, n % 2, p0 - c0:p1 - c0])
                        ins = product(s_ps[g % 2][:, p0:p1], [(qi, ki)])
                ins.then_inc(s_qk, 1)

            def transpose_weights(g):
                i = g % NI
                need(s_norm, g + 1)
                for bank in range((i + 4) // 4):
                    tb = t_banks_through(g - 1) + bank
                    if tb == 0:
                        need(s_bcol, 1)
                    if tb >= 2:
                        need(s_tlo, tb - 1)
                    for kt in range(4 * bank, min(4 * bank + 4, i + 1)):
                        ins = eng.transpose(t_ps[tb % 2][:, (kt % 4) * P:(kt % 4 + 1) * P],
                                            prob[:, g % 3, kt * P:(kt + 1) * P], ident[:, :])
                    ins.then_inc(s_t, 1)

            def weights_times_v(n, kc, second):
                ck = n * NK + kc
                need(s_tlo, t_banks_through(n * NI + 2 * kc + 1))
                need_out(need, ("V", n // 2, 3))
                need(s_olo, ck)
                last = 2 * kc + 1
                for kt in range(kc + 1, last + 1) if second else range(kc + 1):
                    c0 = P if kt == last else 0
                    vi = parts(v, lambda t: t[:, n // 2 % 2, kt, (n % 2) * DH:(n % 2 + 1) * DH])
                    pi = parts(pT[kc % 2], lambda t: t[:, kt, c0:QC])
                    for s, m in HILO:
                        ins = eng.matmul(o_ps[:, c0:QC], vi[s], pi[m], start=(kt == 0 and (s, m) == HILO[0]),
                                         stop=(kt == last and (s, m) == HILO[-1]))
                if second:
                    ins.then_inc(s_pv, 1)

            for piece in before:
                issue_piece(piece)
            for g in range(LAST + 1):
                if g < NG:
                    scores(g)
                for piece in early[g]:
                    issue_piece(piece)
                j = g - PV_LAG
                if 0 <= j < NG:
                    weights_times_v(j // NI, (j % NI) // 2, j % 2 == 1)
                for piece in late[g]:
                    issue_piece(piece)
                if 0 <= g - T_LAG < NG:
                    transpose_weights(g - T_LAG)


_INS = ["L0_attn_x", "L0_attn_Wq", "L0_attn_bq", "L0_attn_Wk", "L0_attn_bk", "L0_attn_Wv", "L0_attn_bv",
        "L0_attn_Wo", "L0_attn_bo", "L0_ffn_w_gate", "L0_ffn_w_up", "L0_ffn_w_down"]


def kernel(**inputs):
    import concourse.bacc as bacc
    from concourse.bass_utils import run_bass_kernel_spmd

    nc = bacc.Bacc("TRN2", target_bir_lowering=False, num_devices=1)
    arrays, args = {}, []
    for name in _INS:
        arr = np.ascontiguousarray(inputs[name])
        arrays[f"in_{name}"] = arr
        args.append(nc.dram_tensor(f"in_{name}", arr.shape, mybir.dt.from_np(arr.dtype), kind="ExternalInput").ap())
    out = nc.dram_tensor("out_0", (B, T, D), F32, kind="ExternalOutput").ap()
    attention_ffn_block(nc, *args, out)
    r = run_bass_kernel_spmd(nc, [arrays], core_ids=[0])
    return r.results[0]["out_0"]
```

```python
from contextlib import ExitStack

import numpy as np

import concourse.bass as bass
from concourse import mybir

F32 = mybir.dt.float32
F32R = mybir.dt.float32r
ALU = mybir.AluOpType
ACT = mybir.ActivationFunctionType
AX_X = mybir.AxisListType.X

P = 128
B, T, D = 4, 1024, 256
NH, DH = 16, 128
HD = NH * DH
HID = 1024
KT = D // P
BANK = 512
EPS = 1e-5
SCALE = float(np.float32(1.0) / np.sqrt(np.float32(DH)))
MASKED = -1e30

CH = 512
NC = B * T // CH
CT = CH // P
NT = B * T // P
HT = HID // P

NHD = B * NH
NI = T // P
NG = NHD * NI
VT = BANK // P
NV = NI // VT
NY = NI // 2
QC = 2 * P
GROUP = 4
QTOK = T // NH
RQ = T // QTOK
T_LAG = 2
PV_AT = {7: (0, 0, 1), 8: (0, 1, 4), 11: (1, 0, 2), 12: (1, 2, 4), 13: (1, 4, 8)}
LAST = NG + NI - 1

HILO = ((0, 0), (0, 1), (1, 0))

T_BANKS = [sum((j + 4) // 4 for j in range(i + 1)) for i in range(NI)]


def t_banks_through(g):
    return T_BANKS[-1] * (g // NI) + T_BANKS[g % NI] if g >= 0 else 0


def pv_parts(g):
    n, i = divmod(g, NI)
    return [(n - back, *PV_AT[i + back * NI]) for back in (1, 0) if i + back * NI in PV_AT and 0 <= n - back < NHD]


def pv_count(n, step):
    return n * len(PV_AT) + sum(at <= step for at in PV_AT)


def pv_chunk(n, kc):
    return pv_count(n, max(at for at, part in PV_AT.items() if part[0] == kc))


def pv_key_tile(n, kt):
    return pv_count(n, max(at for at, (_, k0, k1) in PV_AT.items() if k0 <= kt < k1))


def chunks_done(g):
    return [(n, kc) for n, kc, _, k1 in pv_parts(g) if k1 == VT * (kc + 1)]


def weight_slots(i, bank):
    tiles = list(range(VT * bank, min(VT * (bank + 1), i + 1)))
    return tiles[::-1] if bank else tiles


def score_cols(i):
    L = (i + 1) * P
    c0 = 0 if L <= BANK else BANK - L // 2
    return c0, c0 + L


E, L = 0, 1
K_AT = [((0, E), (1, E)), ((2, E), (3, E)), ((0, E), (1, E)), ((0, L), (6, E))]
V_AT = [((6, E),), ((1, E), (6, E), (7, E)), ((4, L), (5, L), (6, E)), ((7, E),)]
V_AT_BATCH_END = ((5, E), (5, L), (7, E), (8, L))
Q_AT = ((1, E), (1, L), (2, E), (2, L), (3, E), (3, L), (4, E), (4, L))
Y_AT = ((2, L), (3, L), (7, E), (8, E))
Y_LAST = (7, L)


def plan_pieces():
    before = [("Q", 0, m) for m in range(8)] + [("K", 0, 0), ("K", 0, 1)] + [("V", 0, m) for m in range(4)]
    early = {g: [] for g in range(LAST + 1)}
    late = {g: [] for g in range(LAST + 1)}

    def put(what, j, start, places, first=0):
        for m, (i, where) in enumerate(places, first):
            (early, late)[where][start + i].append((what, j, m))

    for pair in range(NHD // 2):
        start = (2 * pair + 2) * NI
        put("y", pair, start, Y_AT if start < NG else Y_AT[:3] + (Y_LAST,))
    for n in range(NHD - 1):
        r, pair, start = n % GROUP, n // 2, n * NI
        put("K", n + 1, start, K_AT[r])
        if n % NH == NH - 1:
            put("V", pair + 1, start, V_AT_BATCH_END)
        elif n % NH != NH - 2:
            put("V", pair + 1, start, V_AT[r], len(V_AT[r - 1]) if r % 2 else 0)
        if r == GROUP - 1:
            put("Q", n // GROUP + 1, start, Q_AT)
    order, bank = list(before), {}
    for j, piece in enumerate(before):
        bank[piece] = ("m", 0, 1)[j % 3]
    for g in range(LAST + 1):
        order += early[g] + late[g]
        for piece in early[g] + late[g]:
            bank[piece] = g % 2 if piece in early[g] and g < NG and g % NI < 4 else "m"
    return before, early, late, order, bank


def plan_splits():
    before = [("Wk", 0), ("Wv", 0), ("Wk", 1)]
    at = {}
    for n in range(NHD):
        r = n % 2
        if n + 2 < NHD:
            at.setdefault((n, 1), []).append(("Wk", n + 2))
        if r == 0 and n // 2 + 1 < NHD // 2:
            at.setdefault((n, 2), []).append(("Wv", n // 2 + 1))
        if r == 1:
            at.setdefault((n, 3), []).append(("Wo", n // 2))
    order = list(before)
    for key in sorted(at):
        order += at[key]
    return before, at, {s: j for j, s in enumerate(order)}


def attention_ffn_block(nc, x, Wq, bq, Wk, bk, Wv, bv, Wo, bo, w_gate, w_up, w_down, out):
    before, early, late, pieces, bank_of = plan_pieces()
    piece_no = {piece: j for j, piece in enumerate(pieces)}
    out_count, before_in_bank, made, latest = {}, {}, {"Q": 0, "other": 0}, {}
    for piece in pieces:
        kind = "Q" if piece[0] == "Q" else "other"
        made[kind] += 1
        out_count[piece] = made[kind]
        before_in_bank[piece] = latest.get(bank_of[piece])
        latest[bank_of[piece]] = piece
    splits_before, splits_at, split_no = plan_splits()
    hi_count, c = {}, 0
    for piece in pieces:
        c += piece[0] in "KV"
        hi_count[piece] = c

    xnT_dram = nc.dram_tensor("xnT_dram", [B, 2, P, KT, T], F32, kind="Internal").ap()
    base_dram = nc.dram_tensor("base_dram", [B * T, D], F32, kind="Internal").ap()

    x_rows = x.rearrange("b t d -> (b t) d").rearrange("(n p) d -> p n d", p=P)
    base_rows = base_dram.rearrange("(n p) d -> p n d", p=P)
    out_rows = out.rearrange("b t d -> (b t) d").rearrange("(n p) d -> p n d", p=P)
    Wq_rows = Wq.rearrange("(k p) n -> p k n", p=P)
    Wk_rows = Wk.rearrange("(k p) n -> p k n", p=P)
    Wv_rows = Wv.rearrange("(k p) n -> p k n", p=P)
    Wo_rows = Wo.rearrange("(h p) n -> p h n", p=P)

    ctx = ExitStack()
    with ctx:
        def sb(name, shape, dt, where=ctx):
            return where.enter_context(nc.sbuf_tensor(name, shape, dt))

        def sb2(name, shape, where=ctx):
            return [sb(f"{name}_{part}", shape, F32R, where) for part in ("hi", "lo")]

        def sem(name):
            return ctx.enter_context(nc.semaphore(name))

        ident = sb("ident", [P, P], F32)
        mask = sb("mask", [P, P], F32)
        bias_rows = sb("bias_rows", [3 * NH, P], F32)
        bias = sb("bias", [P, 3 * NH], F32)
        bqs_sb = sb("bqs_sb", [P, RQ], F32)
        bq_sb, bk_sb, bv_sb = (bias[:, j * NH:(j + 1) * NH] for j in range(3))

        a = ExitStack()
        raw_w = sb("raw_w", [P, 3 * KT * HID], F32, a)
        sil = sb("sil", [P, 2, CH], F32, a)
        y_stage = sb("y_stage", [P, 2, 2, D], F32, a)
        wgT = sb2("wgT", [P, KT, HID], a)
        wuT = sb2("wuT", [P, KT, HID], a)
        xnT_a = sb2("xnT_a", [P, 2, KT, CH], a)
        wdT = sb2("wdT", [P, HT, D], a)
        x_sb = sb("x_sb", [P, NT, D], F32, a)
        hid = sb2("hid", [P, 2, HT, CH], a)
        xn_sb = sb("xn_sb", [P, CT, D], F32, a)
        bo_sb = sb("bo_sb", [P, D], F32, a)
        stats = sb("stats", [P, CT, 6], F32, a)
        mean_var = sb("mean_var", [P, NT, 2], F32, a)
        var_eps = sb("var_eps", [P, NT], F32, a)
        std = sb("std", [P, NT], F32, a)
        rstd = sb("rstd", [P, NT], F32, a)
        newton = sb("newton", [P, NT], F32, a)
        a.close()
        wg_raw = raw_w[:, 0:KT * HID].rearrange("p (n d) -> p n d", d=D)
        wu_raw = raw_w[:, KT * HID:2 * KT * HID].rearrange("p (n d) -> p n d", d=D)
        wd_raw = raw_w[:, 2 * KT * HID:3 * KT * HID].rearrange("p (n h) -> p n h", h=HID)
        wq_raw = raw_w[:, 0:KT * HD].rearrange("p (k n) -> p k n", k=KT)

        v = sb2("v", [P, 2, NI, 2 * DH])
        wq = sb2("wq", [P, KT, HD])
        xnT = sb2("xnT", [P, KT, T])
        qT = sb("qT", [P, GROUP, T], F32)
        q = sb2("q", [P, 2, BANK])
        k = sb2("k", [P, 2, T])
        prob = sb("prob", [P, 3, T], F32)
        pT_full = sb2("pT_full", [P, VT, BANK])
        pT_diag = sb2("pT_diag", [P, VT * (VT + 1), P])
        oT_even = sb2("oT_even", [P, T])
        oT_odd = sb2("oT_odd", [P, BANK])
        y = sb("y", [P, NI, D], F32)
        wk_raw = sb("wk_raw", [P, 2, KT, DH], F32)
        wk = sb2("wk", [P, 2, KT, DH])
        wv_raw = sb("wv_raw", [P, KT, 2 * DH], F32)
        wv = sb2("wv", [P, KT, 2 * DH])
        wo_raw = sb("wo_raw", [P, 2, D], F32)
        wo = sb2("wo", [P, 2, D])
        neg_max = sb("neg_max", [P, 4], F32)
        row_sum = sb("row_sum", [P, 4], F32)
        inv_sum = sb("inv_sum", [P, 4], F32)

        def pb(name, cols):
            return ctx.enter_context(nc.psum_tensor(name, [P, cols], F32))

        s_ps = [pb("s_ps0", 2 * BANK), pb("s_ps1", 2 * BANK)]
        t_ps = [pb("t_ps0", BANK), pb("t_ps1", BANK)]
        o_ps = pb("o_ps", BANK)
        m_ps = pb("m_ps", BANK)

        s_x = [sem(f"s_x{n}") for n in range(NC)]
        s_wg, s_wu = ([sem(f"s_{w}{half}") for half in range(2)] for w in ("wg", "wu"))
        s_wd, s_wqraw = sem("s_wd"), sem("s_wqraw")
        s_bias, s_bo = sem("s_bias"), sem("s_bo")
        s_xst = [sem("s_xst0"), sem("s_xst1")]
        s_yst = [sem("s_yst0"), sem("s_yst1")]
        s_xload = [sem("s_xload_hi"), sem("s_xload_lo")]
        s_wkraw = [sem("s_wkraw0"), sem("s_wkraw1")]
        s_wvraw, s_woraw = sem("s_wvraw"), sem("s_woraw")
        s_base = [sem(f"s_base{j}") for j in range(NY)]
        s_out = [sem(f"s_out{j}") for j in range(NY)]
        s_const, s_biasT, s_bcol, s_bqs = sem("s_const"), sem("s_biasT"), sem("s_bcol"), sem("s_bqs")
        s_stat = sem("s_stat")
        s_veps = sem("s_veps")
        s_std = sem("s_std")
        s_xn = sem("s_xn")
        s_ta = sem("s_ta")
        s_tahi = sem("s_tahi")
        s_talo = sem("s_talo")
        s_gate, s_up = sem("s_gate"), sem("s_up")
        s_silu, s_h = sem("s_silu"), sem("s_h")
        s_hidhi, s_hid = sem("s_hidhi"), sem("s_hid")
        s_xbo = sem("s_xbo")
        s_down = sem("s_down")
        s_ffn = sem("s_ffn")
        s_wqhi, s_wq = sem("s_wqhi"), sem("s_wq")
        s_qk = sem("s_qk")
        s_masked = sem("s_masked")
        s_max = sem("s_max")
        s_exp = sem("s_exp")
        s_inv = sem("s_inv")
        s_norm = sem("s_norm")
        s_t = sem("s_t")
        s_thi, s_tlo = sem("s_thi"), sem("s_tlo")
        s_pv = sem("s_pv")
        s_ohi, s_olo = sem("s_ohi"), sem("s_olo")
        s_fill = sem("s_fill")
        s_fillhi = sem("s_fillhi")
        s_qout, s_pout = sem("s_qout"), sem("s_pout")
        s_qhi, s_q = sem("s_qhi"), sem("s_q")
        s_splithi, s_split = sem("s_splithi"), sem("s_split")

        def waits(eng):
            seen = {}

            def need(s, count):
                if count > seen.get(id(s), 0):
                    seen[id(s)] = count
                    eng.wait_ge(s, count)
            return need

        def need_out(need, piece):
            need(s_qout if piece[0] == "Q" else s_pout, out_count[piece])

        def piece_ps(piece):
            where = bank_of[piece]
            return m_ps[:, :] if where == "m" else s_ps[where][:, BANK:2 * BANK]

        a_first = [("wg", 0, 0), ("wg", 1, 0), ("x", 0, 0), ("x", 0, 1), ("wu", 0, 0), ("wu", 1, 0)]
        a_after = {(0, 0): [("wg", 0, 1), ("wg", 1, 1)], (0, 1): [("wu", 0, 1), ("wu", 1, 1)],
                   (0, 2): [("wd", 0), ("wd", 1)], (0, 4): [("wd", 2), ("wd", 3)]}
        for c in range(NC - 1):
            a_after[c, 3] = [("x", c + 1, kt) for kt in range(KT)]
        a_banks = a_first + [b for key in sorted(a_after) for b in a_after[key]]
        a_bank_no = {b: j for j, b in enumerate(a_banks)}
        A_WIDE = 8

        def a_ps(j):
            return (t_ps[0], t_ps[1], o_ps, m_ps)[j % 4] if j < A_WIDE else t_ps[j % 2]

        def a_copied_before(j):
            return j - 3 if j < A_WIDE else j - 1

        def a_dst(b, part):
            if b[0] == "x":
                return xnT_a[part][:, b[1] % 2, b[2], :]
            if b[0] == "wd":
                return wdT[part][:, 2 * b[1]:2 * b[1] + 2, :].rearrange("p n d -> p (n d)")
            _, kt, half = b
            return (wgT if b[0] == "wg" else wuT)[part][:, kt, half * BANK:(half + 1) * BANK]

        def pT_written(t, i, bank):
            if bank:
                i -= VT
                return t["diag"][:, (VT - 1) * (VT + 1) - VT * i - i:(VT - 1) * (VT + 1) + i + 1:VT + 2, :]
            if i >= VT:
                return t["full"][:, :, (i - VT) * P:(i - VT + 1) * P]
            return t["diag"][:, 1 + i:1 + i + VT * i + i + 1:VT + 1, :]

        def pT_read(t, kc, kt):
            if kt < VT * kc:
                return t["full"][:, kt, :]
            k = kt - VT * kc
            first = (VT - 1 - k) * (VT + 1) if kc else k * (VT + 1) + 1 + k
            return t["diag"][:, first:first + VT - k, :].rearrange("p n t -> p (n t)")

        def t_ps_used(tb, i, bank):
            cols = len(weight_slots(i, bank)) * P
            return t_ps[tb % 2][:, 0:cols].rearrange("p (n t) -> p n t", t=P)

        pT = [{"full": pT_full[part], "diag": pT_diag[part]} for part in range(2)]

        def o_slot(n, kc):
            pair = n // 2
            if n % 2 == 0:
                last_read = ("y", pair - 1, 2 * kc + 1)
                dst = [t[:, kc * BANK:(kc + 1) * BANK] for t in oT_even]
            else:
                last_read = ("y", pair, 1) if kc else ("y", pair - 1, 3)
                dst = [t[:, :] for t in oT_odd]
            return dst, (last_read if last_read[1] >= 0 else None)

        std_groups = [(0, 1), (1, 2), (2, NC)]

        block = ctx.enter_context(nc.Block())

        @block.sync
        def _(eng):
            need = waits(eng)

            def load_x(c):
                eng.dma_start(x_sb[:, c * CT:(c + 1) * CT, :], x_rows[:, c * CT:(c + 1) * CT, :]).then_inc(s_x[c], 16)

            def load_half(raw, w, half, done):
                n = slice(half * HT // 2, (half + 1) * HT // 2)
                eng.dma_start(raw[:, n, :], w.rearrange("(n p) d -> p n d", p=P)[:, n, :]).then_inc(done[half], 16)

            load_x(0)
            for half in range(2):
                load_half(wg_raw, w_gate, half, s_wg)
                load_half(wu_raw, w_up, half, s_wu)
            load_x(1)
            eng.dma_start(wd_raw, w_down.rearrange("(n p) h -> p n h", p=P)).then_inc(s_wd, 16)
            eng.dma_start(bo_sb[:, :], bo.partition_broadcast(P)).then_inc(s_bo, 16)
            for c in range(2, NC):
                load_x(c)
            for j, src in enumerate((bq, bk, bv)):
                eng.dma_start(bias_rows[j * NH:(j + 1) * NH, :], src.rearrange("(h p) -> h p", p=P)).then_inc(s_bias, 16)

            def store_xnT(c):
                need(s_talo, a_bank_no[("x", c, KT - 1)] + 1)
                b, half = divmod(c, T // CH)
                for part in range(2):
                    eng.dma_start(xnT_dram[b, part][:, :, half * CH:(half + 1) * CH],
                                  xnT_a[part][:, c % 2, :, :].bitcast(F32)).then_inc(s_xst[c % 2], 16)

            def store_base(c):
                for d in range(2):
                    need(s_ffn, 2 * c + d + 1)
                    t0 = c * CT + 2 * d
                    eng.dma_start(base_rows[:, t0:t0 + 2, :], y_stage[:, d, :, :]).then_inc(s_yst[d], 16)

            store_xnT(0)
            for c in range(NC):
                if c + 1 < NC:
                    store_xnT(c + 1)
                if c == 0:
                    need(s_ta, a_bank_no[("wd", 3)] + 1)
                    eng.dma_start(wq_raw, Wq_rows).then_inc(s_wqraw, 16)
                if c >= 1:
                    store_base(c - 1)

            def load_xnT(b):
                for part in range(2):
                    eng.dma_start(xnT[part][:, :, :].bitcast(F32), xnT_dram[b, part]).then_inc(s_xload[part], 16)

            need(s_up, NC * HT)
            for slot in range(2):
                need(s_xst[slot], 32 * (NC // 2))
            load_xnT(0)
            store_base(NC - 1)
            need(s_down, 2 * NC)
            need(s_ffn, 2 * NC)

            def load_wk(n):
                h = n % NH
                if n >= 2:
                    need(s_split, split_no[("Wk", n - 2)] + 1)
                eng.dma_start(wk_raw[:, n % 2, :, :], Wk_rows[:, :, h * DH:(h + 1) * DH]).then_inc(s_wkraw[n % 2], 16)

            def load_wv(pair):
                h = 2 * pair % NH
                if pair >= 1:
                    need(s_split, split_no[("Wv", pair - 1)] + 1)
                eng.dma_start(wv_raw[:, :, :], Wv_rows[:, :, h * DH:(h + 2) * DH]).then_inc(s_wvraw, 16)

            def load_wo(pair):
                h = 2 * pair % NH
                if pair >= 1:
                    need(s_split, split_no[("Wo", pair - 1)] + 1)
                eng.dma_start(wo_raw[:, :, :], Wo_rows[:, h:h + 2, :]).then_inc(s_woraw, 16)

            def load_base(b, j):
                if b >= 1:
                    need(s_out[j], 16 * b)
                t0 = b * NI + 2 * j
                eng.dma_start(y[:, 2 * j:2 * j + 2, :], base_rows[:, t0:t0 + 2, :]).then_inc(s_base[j], 16)

            def store_out(b, j):
                need_out(need, ("y", (b + 1) * NH // 2 - 1, j))
                t0 = b * NI + 2 * j
                eng.dma_start(out_rows[:, t0:t0 + 2, :], y[:, 2 * j:2 * j + 2, :]).then_inc(s_out[j], 16)

            load_wk(0)
            load_wv(0)
            load_wk(1)
            load_wo(0)
            for slot in range(2):
                need(s_yst[slot], 16 * NC)
            for j in range(NY):
                load_base(0, j)
            for n in range(NHD):
                b = n // NH
                if n + 2 < NHD:
                    load_wk(n + 2)
                if n % 2 == 0 and n // 2 + 1 < NHD // 2:
                    load_wv(n // 2 + 1)
                if n % 2 == 0 and n:
                    load_wo(n // 2)
                if n % NH == 0 and n:
                    for j in range(NY):
                        store_out(b - 1, j)
                        load_base(b, j)
                if n % NH == NH - 2 and b + 1 < B:
                    need(s_fill, piece_no[("K", n + 1, 1)] + 1)
                    load_xnT(b + 1)
            for j in range(NY):
                store_out(B - 1, j)
            for j in range(NY):
                need(s_out[j], 16 * B)

        @block.gpsimd
        def _(eng):
            need = waits(eng)
            eng.memset(ident[:, :], 0.0).then_inc(s_const, 1)
            eng.memset(mask[:, :], 0.0).then_inc(s_const, 1)
            need(s_const, 2)
            eng.affine_select(out=ident[:, :], in_=ident[:, :], compare_op=ALU.not_equal, fill=1.0,
                              base=0, pattern=[[-1, P]], channel_multiplier=1).then_inc(s_const, 1)
            eng.affine_select(out=mask[:, :], in_=mask[:, :], compare_op=ALU.is_ge, fill=MASKED,
                              base=0, pattern=[[-1, P]], channel_multiplier=1).then_inc(s_const, 1)

            count = {}

            def split(dst, src, sem_hi, sem_lo, index):
                count[id(sem_hi)] = count.get(id(sem_hi), 0) + 1
                eng.tensor_scalar(index(dst[0]), src, 1.0, 1.0, ALU.mult, ALU.mult).then_inc(sem_hi, 1)
                need(sem_hi, count[id(sem_hi)])
                eng.tensor_tensor(index(dst[1]), src, index(dst[0]), ALU.subtract).then_inc(sem_lo, 1)

            for c in range(NC):
                for ht in range(HT):
                    u = c * HT + ht
                    if ht == 0:
                        need(s_xn, c + 1)
                        need(s_bo, 16)
                        for t in range(c * CT, (c + 1) * CT):
                            ins = eng.tensor_tensor(x_sb[:, t, :], x_sb[:, t, :], bo_sb[:, :], ALU.add)
                        ins.then_inc(s_xbo, 1)
                        if c >= 2:
                            need(s_down, 2 * (c - 1))
                    need(s_h, u + 1)
                    split(hid, sil[:, u % 2, :], s_hidhi, s_hid, lambda t: t[:, c % 2, ht, :])

            need(s_wqraw, 16)
            need(s_up, NC * HT)
            for kt in range(KT):
                for half in range(2):
                    cols = slice(half * HD // 2, (half + 1) * HD // 2)
                    split(wq, wq_raw[:, kt, cols], s_wqhi, s_wq, lambda t: t[:, kt, cols])
            need(s_down, 2 * NC)
            need(s_ffn, 2 * NC)

            def split_weight(which):
                what, j = which
                if what == "Wk":
                    need(s_wkraw[j % 2], 16 * (j // 2 + 1))
                    if j >= 2:
                        need(s_fill, piece_no[("K", j - 2, 1)] + 1)
                    split(wk, wk_raw[:, j % 2, :, :], s_splithi, s_split, lambda t: t[:, j % 2, :, :])
                elif what == "Wv":
                    need(s_wvraw, 16 * (j + 1))
                    if j:
                        need(s_fill, piece_no[("V", j - 1, 3)] + 1)
                    split(wv, wv_raw[:, :, :], s_splithi, s_split, lambda t: t[:, :, :])
                else:
                    need(s_woraw, 16 * (j + 1))
                    if j:
                        need(s_fill, piece_no[("y", j - 1, NY - 1)] + 1)
                    split(wo, wo_raw[:, :, :], s_splithi, s_split, lambda t: t[:, :, :])

            def split_q(n, half):
                need_out(need, ("Q", n // GROUP, 7))
                if n:
                    need(s_qk, NI * (n - 1) + 4 * (half + 1))
                split(q, qT[:, n % GROUP, half * BANK:(half + 1) * BANK], s_qhi, s_q, lambda t: t[:, half, :])

            for which in splits_before:
                split_weight(which)
            split_q(0, 0)
            for g in range(NG + 1):
                if g >= 1:
                    j, L = g - 1, ((g - 1) % NI + 1) * P
                    need(s_inv, j + 1)
                    eng.tensor_scalar(prob[:, j % 3, 0:L], prob[:, j % 3, 0:L], inv_sum[:, j % 4:j % 4 + 1], 1.0,
                                      ALU.mult, ALU.mult).then_inc(s_norm, 1)
                if g == NG:
                    break
                n, i = divmod(g, NI)
                if i == 0:
                    split_q(n, 1)
                for which in splits_at.get((n, i), []):
                    split_weight(which)
                if i == 5 and n + 1 < NHD:
                    split_q(n + 1, 0)

        @block.scalar
        def _(eng):
            need = waits(eng)

            def roots(j):
                t0, t1 = std_groups[j][0] * CT, std_groups[j][1] * CT
                need(s_veps, j + 1)
                eng.activation(std[:, t0:t1], var_eps[:, t0:t1], ACT.Sqrt).then_inc(s_std, 1)

            def part_hi(b):
                j = a_bank_no[b]
                need(s_ta, j + 1)
                if b[0] == "x" and b[1] >= 2:
                    need(s_up, (b[1] - 1) * HT)
                    need(s_xst[b[1] % 2], 32 * (b[1] // 2))
                eng.activation(a_dst(b, 0), a_ps(j)[:, :], ACT.Copy).then_inc(s_tahi, 1)

            roots(0)
            for b in a_first:
                part_hi(b)
            for c in range(NC):
                for ht in range(HT):
                    u = c * HT + ht
                    need(s_gate, u + 1)
                    if u >= 2:
                        need(s_hid, u - 1)
                    eng.activation(sil[:, u % 2, :], s_ps[u % 2][:, 0:CH], ACT.Silu).then_inc(s_silu, 1)
                    if ht == 1 and c + 1 < len(std_groups):
                        roots(c + 1)
                    for b in a_after.get((c, ht), []):
                        part_hi(b)

            need(s_biasT, 1)
            eng.activation(bias[:, :], t_ps[0][:, 0:3 * NH], ACT.Copy).then_inc(s_bcol, 1)
            need(s_bcol, 1)
            eng.activation(bqs_sb[:, :], bq_sb, ACT.Copy, scale=SCALE).then_inc(s_bqs, 1)
            need(s_bqs, 1)
            need(s_ffn, 2 * NC)
            need(s_hid, NC * HT)
            for slot in range(2):
                need(s_yst[slot], 16 * NC)

            def piece_out(piece):
                what, j, m = piece
                ps = piece_ps(piece)
                if what == "y":
                    return
                need(s_fill, piece_no[piece] + 1)
                if what == "K":
                    if j >= 2:
                        need(s_qk, NI * (j - 1))
                    h = j % NH
                    eng.activation(k[0][:, j % 2, m * BANK:(m + 1) * BANK], ps, ACT.Identity,
                                   bias=bk_sb[:, h:h + 1]).then_inc(s_fillhi, 1)
                elif what == "V":
                    need(s_wq, 4)
                    if j >= 2:
                        need(s_pv, pv_key_tile(2 * j - 3, 2 * m + 1))
                    eng.activation(v[0][:, j % 2, 2 * m:2 * m + 2, :].rearrange("p n d -> p (n d)"), ps,
                                   ACT.Copy).then_inc(s_fillhi, 1)
                else:
                    if j:
                        need(s_q, 2 * GROUP * j)
                    for c2 in range(2):
                        c = 2 * m + c2
                        dst = qT[:, :, :].rearrange("p h (r c) -> p c h r", c=RQ)[:, c]
                        src = ps[:, c2 * QC:(c2 + 1) * QC].rearrange("p (h r) -> p h r", h=GROUP)
                        ins = eng.activation(dst, src, ACT.Identity, bias=bqs_sb[:, c:c + 1], scale=SCALE)
                    ins.then_inc(s_qout, 1)

            for piece in before:
                piece_out(piece)
            for g in range(LAST + 1):
                j = g - 1
                if 0 <= j < NG:
                    L = (j % NI + 1) * P
                    need(s_max, j + 1)
                    if j >= 3:
                        need(s_t, t_banks_through(j - 3))
                    c0, c1 = score_cols(j % NI)
                    eng.activation(prob[:, j % 3, 0:L], s_ps[j % 2][:, c0:c1], ACT.Exp,
                                   bias=neg_max[:, j % 4:j % 4 + 1],
                                   accum_out=row_sum[:, j % 4:j % 4 + 1]).then_inc(s_exp, 1)
                for piece in early[g]:
                    piece_out(piece)
                for n, kc in chunks_done(g):
                    need(s_pv, pv_chunk(n, kc))
                    dst, last_read = o_slot(n, kc)
                    if last_read:
                        need(s_fill, piece_no[last_read] + 1)
                    h = n % NH
                    eng.activation(dst[0], o_ps[:, :], ACT.Identity, bias=bv_sb[:, h:h + 1]).then_inc(s_ohi, 1)
                for piece in late[g]:
                    piece_out(piece)
                j = g - T_LAG
                if 0 <= j < NG:
                    n, i = divmod(j, NI)
                    if n:
                        need(s_pv, pv_chunk(n - 1, i // VT))
                    for bank in range(i // VT + 1):
                        tb = t_banks_through(j - 1) + bank
                        need(s_t, tb + 1)
                        eng.activation(pT_written(pT[0], i, bank), t_ps_used(tb, i, bank), ACT.Copy)\
                           .then_inc(s_thi, 1)

        @block.vector
        def _(eng):
            need = waits(eng)
            chain = [0]

            def link(ins):
                chain[0] += 1
                ins.then_inc(s_stat, 1)
                need(s_stat, chain[0])

            def statistics(c):
                need(s_x[c], 16)
                for t in range(CT):
                    ins = eng.bn_stats(stats[:, t, :], x_sb[:, c * CT + t, :])
                link(ins)
                for t in range(CT):
                    ins = eng.bn_aggr(mean_var[:, c * CT + t, :], stats[:, t, :])
                link(ins)

            def plus_eps(j):
                t0, t1 = std_groups[j][0] * CT, std_groups[j][1] * CT
                eng.tensor_scalar(var_eps[:, t0:t1], mean_var[:, t0:t1, 1], EPS, None, ALU.add).then_inc(s_veps, 1)

            def inverse_std(j):
                t0, t1 = std_groups[j][0] * CT, std_groups[j][1] * CT
                r, w, s = rstd[:, t0:t1], newton[:, t0:t1], var_eps[:, t0:t1]
                need(s_veps, j + 1)
                need(s_std, j + 1)
                link(eng.reciprocal(r, std[:, t0:t1]))
                link(eng.tensor_tensor(w, r, r, ALU.mult))
                link(eng.tensor_tensor(w, w, s, ALU.mult))
                link(eng.tensor_scalar(w, w, -0.5, 1.5, ALU.mult, ALU.add))
                link(eng.tensor_tensor(r, r, w, ALU.mult))

            def normed(c):
                if c:
                    need(s_ta, a_bank_no[("x", c - 1, KT - 1)] + 1)
                for j in range(CT):
                    t = c * CT + j
                    ins = eng.tensor_scalar(xn_sb[:, j, :], x_sb[:, t, :], mean_var[:, t, 0:1], rstd[:, t:t + 1],
                                            ALU.subtract, ALU.mult)
                ins.then_inc(s_xn, 1)

            def part_lo(b):
                j = a_bank_no[b]
                need(s_tahi, j + 1)
                eng.tensor_tensor(a_dst(b, 1), a_ps(j)[:, :], a_dst(b, 0), ALU.subtract).then_inc(s_talo, 1)

            def base_out(c):
                need(s_xbo, c + 1)
                for d in range(2):
                    need(s_down, 2 * c + d + 1)
                    if c:
                        need(s_yst[d], 16 * c)
                    t0 = c * CT + 2 * d
                    eng.tensor_tensor(y_stage[:, d, :, :].rearrange("p n d -> p (n d)"), (o_ps, m_ps)[d][:, :],
                                      x_sb[:, t0:t0 + 2, :].rearrange("p n d -> p (n d)"), ALU.add).then_inc(s_ffn, 1)

            statistics(0)
            plus_eps(0)
            inverse_std(0)
            normed(0)
            for b in a_first:
                part_lo(b)
            for c in range(NC):
                for ht in range(HT):
                    u = c * HT + ht
                    if c == 0 and ht == 1:
                        statistics(1)
                        plus_eps(1)
                    if c == 0 and ht >= 3:
                        statistics(ht - 1)
                    if c == 1 and ht == 0:
                        statistics(NC - 1)
                        plus_eps(2)
                    need(s_up, u + 1)
                    need(s_silu, u + 1)
                    eng.tensor_tensor(sil[:, u % 2, :], sil[:, u % 2, :], s_ps[u % 2][:, CH:2 * CH], ALU.mult)\
                       .then_inc(s_h, 1)
                    if ht == 1 and c + 1 < len(std_groups):
                        inverse_std(c + 1)
                    if ht == 2 and c + 1 < NC:
                        normed(c + 1)
                    for b in a_after.get((c, ht), []):
                        part_lo(b)
                if c >= 1:
                    base_out(c - 1)
            base_out(NC - 1)

            need(s_bcol, 1)
            need(s_const, 4)
            need(s_hid, NC * HT)
            for slot in range(2):
                need(s_yst[slot], 16 * NC)

            def piece_out(piece):
                what, j, m = piece
                ps = piece_ps(piece)
                if what == "Q":
                    return
                if what == "y":
                    b, pair = divmod(j, NH // 2)
                    need(s_fill, piece_no[piece] + 1)
                    need(s_base[m], 16 * (b + 1))
                    if pair:
                        need_out(need, ("y", j - 1, m))
                    rows = y[:, 2 * m:2 * m + 2, :].rearrange("p n d -> p (n d)")
                    eng.tensor_tensor(rows, ps, rows, ALU.add).then_inc(s_pout, 1)
                    return
                need(s_fillhi, hi_count[piece])
                if what == "K":
                    h, cols = j % NH, slice(m * BANK, (m + 1) * BANK)
                    eng.scalar_tensor_tensor(out=k[1][:, j % 2, cols], in0=ps, scalar=bk_sb[:, h:h + 1],
                                             in1=k[0][:, j % 2, cols], op0=ALU.add, op1=ALU.subtract)\
                       .then_inc(s_pout, 1)
                else:
                    hi, lo = (t[:, j % 2, 2 * m:2 * m + 2, :].rearrange("p n d -> p (n d)") for t in v)
                    eng.tensor_tensor(lo, ps, hi, ALU.subtract).then_inc(s_pout, 1)

            for piece in before:
                piece_out(piece)
            for g in range(LAST + 1):
                if g < NG:
                    need(s_qk, g + 1)
                    if g >= 4:
                        need(s_exp, g - 3)
                    c0, c1 = score_cols(g % NI)
                    diagonal = s_ps[g % 2][:, c1 - P:c1]
                    eng.tensor_tensor(diagonal, diagonal, mask[:, :], ALU.add).then_inc(s_masked, 1)
                    need(s_masked, g + 1)
                    eng.tensor_reduce(neg_max[:, g % 4:g % 4 + 1], s_ps[g % 2][:, c0:c1], AX_X, ALU.max,
                                      negate=True).then_inc(s_max, 1)
                for piece in early[g]:
                    piece_out(piece)
                if 1 <= g <= NG:
                    j = g - 1
                    need(s_exp, j + 1)
                    if j >= 4:
                        need(s_norm, j - 3)
                    eng.reciprocal(inv_sum[:, j % 4:j % 4 + 1], row_sum[:, j % 4:j % 4 + 1]).then_inc(s_inv, 1)
                for n, kc in chunks_done(g):
                    need(s_ohi, n * NV + kc + 1)
                    dst, _ = o_slot(n, kc)
                    h = n % NH
                    eng.scalar_tensor_tensor(out=dst[1], in0=o_ps[:, :], scalar=bv_sb[:, h:h + 1], in1=dst[0],
                                             op0=ALU.add, op1=ALU.subtract).then_inc(s_olo, 1)
                for piece in late[g]:
                    piece_out(piece)
                j = g - T_LAG
                if 0 <= j < NG:
                    n, i = divmod(j, NI)
                    for bank in range(i // VT + 1):
                        tb = t_banks_through(j - 1) + bank
                        need(s_thi, tb + 1)
                        hi, lo = (pT_written(t, i, bank) for t in pT)
                        eng.tensor_tensor(lo, t_ps_used(tb, i, bank), hi, ALU.subtract).then_inc(s_tlo, 1)

        @block.tensor
        def _(eng):
            need = waits(eng)

            def product(dst, terms):
                for j, (sta, mov) in enumerate(terms):
                    for s, m in HILO:
                        ins = eng.matmul(dst, sta[s], mov[m], start=(j == 0 and (s, m) == HILO[0]),
                                         stop=(j == len(terms) - 1 and (s, m) == HILO[-1]))
                return ins

            def parts(t, index):
                return [index(t[0]), index(t[1])]

            def transposes(b):
                j = a_bank_no[b]
                need(s_const, 3)
                if b[0] == "x":
                    need(s_xn, b[1] + 1)
                    src = [xn_sb[:, t, b[2] * P:(b[2] + 1) * P] for t in range(CT)]
                elif b[0] == "wd":
                    need(s_wd, 16)
                    src = [wd_raw[:, dt, ht * P:(ht + 1) * P] for ht in (2 * b[1], 2 * b[1] + 1) for dt in range(KT)]
                else:
                    _, kt, half = b
                    need((s_wg if b[0] == "wg" else s_wu)[half], 16)
                    raw = wg_raw if b[0] == "wg" else wu_raw
                    src = [raw[:, 4 * half + ht, kt * P:(kt + 1) * P] for ht in range(4)]
                need(s_talo, a_copied_before(j))
                for c, s in enumerate(src):
                    ins = eng.transpose(a_ps(j)[:, c * P:(c + 1) * P], s, ident[:, :])
                ins.then_inc(s_ta, 1)

            def gate_up(c, ht):
                u = c * HT + ht
                need(s_talo, a_bank_no[("x", c, KT - 1)] + 1)
                if u >= 2:
                    need(s_h, u - 1)
                for w, half, done in ((wgT, 0, s_gate), (wuT, 1, s_up)):
                    name = "wg" if w is wgT else "wu"
                    need(s_talo, a_bank_no[name, KT - 1, 2 * ht // HT] + 1)
                    terms = [(parts(w, lambda t: t[:, kt, ht * P:(ht + 1) * P]),
                              parts(xnT_a, lambda t: t[:, c % 2, kt, :])) for kt in range(KT)]
                    product(s_ps[u % 2][:, half * CH:(half + 1) * CH], terms).then_inc(done, 1)

            def down(c):
                need(s_talo, a_bank_no[("wd", 3)] + 1)
                need(s_hid, (c + 1) * HT)
                for d in range(2):
                    if c:
                        need(s_ffn, 2 * (c - 1) + d + 1)
                    for t2 in range(2):
                        t = 2 * d + t2
                        terms = [(parts(hid, lambda h: h[:, c % 2, ht, t * P:(t + 1) * P]),
                                  parts(wdT, lambda w: w[:, ht, :])) for ht in range(HT)]
                        ins = product((o_ps, m_ps)[d][:, t2 * D:(t2 + 1) * D], terms)
                    ins.then_inc(s_down, 1)

            for b in a_first:
                transposes(b)
            for c in range(NC):
                for ht in range(HT):
                    gate_up(c, ht)
                    for b in a_after.get((c, ht), []):
                        transposes(b)
                if c >= 1:
                    down(c - 1)
            down(NC - 1)

            need(s_bias, 48)
            need(s_talo, len(a_banks))
            eng.transpose(t_ps[0][:, 0:3 * NH], bias_rows[:, :], ident[0:3 * NH, 0:3 * NH]).then_inc(s_biasT, 1)
            need(s_ffn, 2 * NC)

            def issue_piece(piece):
                what, j, m = piece
                ps = piece_ps(piece)
                if before_in_bank[piece]:
                    need_out(need, before_in_bank[piece])
                if what == "y":
                    need(s_split, split_no[("Wo", j)] + 1)
                    need(s_olo, NV * (2 * j + 1) + m // 2 + 1)
                    for t2 in range(2):
                        even = parts(oT_even, lambda t: t[:, (2 * m + t2) * P:(2 * m + t2 + 1) * P])
                        odd = parts(oT_odd, lambda t: t[:, (m % 2 * 2 + t2) * P:(m % 2 * 2 + t2 + 1) * P])
                        terms = [(o, parts(wo, lambda t: t[:, hh, :])) for hh, o in enumerate((even, odd))]
                        ins = product(ps[:, t2 * D:(t2 + 1) * D], terms)
                    ins.then_inc(s_fill, 1)
                    return
                heads_per = {"K": 1, "V": 2, "Q": GROUP}[what]
                for part in range(2):
                    need(s_xload[part], 16 * (j * heads_per // NH + 1))
                if what == "K":
                    need(s_split, split_no[("Wk", j)] + 1)
                    terms = [(parts(wk, lambda t: t[:, j % 2, kt, :]),
                              parts(xnT, lambda t: t[:, kt, m * BANK:(m + 1) * BANK])) for kt in range(KT)]
                    ins = product(ps, terms)
                elif what == "V":
                    need(s_split, split_no[("Wv", j)] + 1)
                    for t2 in range(2):
                        st = 2 * m + t2
                        terms = [(parts(xnT, lambda t: t[:, kt, st * P:(st + 1) * P]),
                                  parts(wv, lambda t: t[:, kt, :])) for kt in range(KT)]
                        ins = product(ps[:, t2 * 2 * DH:(t2 + 1) * 2 * DH], terms)
                else:
                    need(s_wq, 4)
                    tok = j * GROUP % NH * QTOK
                    for c2 in range(2):
                        c = 2 * m + c2
                        terms = [(parts(wq, lambda t: t[:, kt, c * P:(c + 1) * P]),
                                  parts(xnT, lambda t: t[:, kt, tok:tok + QC])) for kt in range(KT)]
                        ins = product(ps[:, c2 * QC:(c2 + 1) * QC], terms)
                ins.then_inc(s_fill, 1)

            def scores(g):
                n, i = divmod(g, NI)
                need_out(need, ("K", n, 1))
                need(s_q, 2 * n + i // 4 + 1)
                if g >= 2:
                    need(s_exp, g - 1)
                if i in (4, 5):
                    for piece in [p for s in range(i - 4, 4, 2) for p in early[n * NI + s]]:
                        need_out(need, piece)
                c0, c1 = score_cols(i)
                qi = parts(q, lambda t: t[:, i // 4, (i % 4) * P:(i % 4 + 1) * P])
                for p0, p1 in ((c0, min(c1, BANK)), (BANK, c1)):
                    if p0 < p1:
                        ki = parts(k, lambda t: t[:, n % 2, p0 - c0:p1 - c0])
                        ins = product(s_ps[g % 2][:, p0:p1], [(qi, ki)])
                ins.then_inc(s_qk, 1)

            def transpose_weights(g):
                i = g % NI
                need(s_norm, g + 1)
                for bank in range(i // VT + 1):
                    tb = t_banks_through(g - 1) + bank
                    if tb == 0:
                        need(s_bcol, 1)
                    if tb >= 2:
                        need(s_tlo, tb - 1)
                    for slot, kt in enumerate(weight_slots(i, bank)):
                        ins = eng.transpose(t_ps[tb % 2][:, slot * P:(slot + 1) * P],
                                            prob[:, g % 3, kt * P:(kt + 1) * P], ident[:, :])
                    ins.then_inc(s_t, 1)

            def weights_times_v(n, kc, k0, k1):
                last = VT * (kc + 1) - 1
                need(s_tlo, t_banks_through(n * NI + last))
                need_out(need, ("V", n // 2, 3))
                need(s_olo, n * NV + kc)
                for kt in range(k0, k1):
                    c0 = max(0, kt - VT * kc) * P
                    vi = parts(v, lambda t: t[:, n // 2 % 2, kt, (n % 2) * DH:(n % 2 + 1) * DH])
                    pi = [pT_read(t, kc, kt) for t in pT]
                    for s, m in HILO:
                        ins = eng.matmul(o_ps[:, c0:BANK], vi[s], pi[m], start=(kt == 0 and (s, m) == HILO[0]),
                                         stop=(kt == last and (s, m) == HILO[-1]))
                ins.then_inc(s_pv, 1)

            for piece in before:
                issue_piece(piece)
            for g in range(LAST + 1):
                if g < NG:
                    scores(g)
                for piece in early[g]:
                    issue_piece(piece)
                for part in pv_parts(g):
                    weights_times_v(*part)
                for piece in late[g]:
                    issue_piece(piece)
                if 0 <= g - T_LAG < NG:
                    transpose_weights(g - T_LAG)


_INS = ["L0_attn_x", "L0_attn_Wq", "L0_attn_bq", "L0_attn_Wk", "L0_attn_bk", "L0_attn_Wv", "L0_attn_bv",
        "L0_attn_Wo", "L0_attn_bo", "L0_ffn_w_gate", "L0_ffn_w_up", "L0_ffn_w_down"]


def kernel(**inputs):
    import concourse.bacc as bacc
    from concourse.bass_utils import run_bass_kernel_spmd

    nc = bacc.Bacc("TRN2", target_bir_lowering=False, num_devices=1)
    arrays, args = {}, []
    for name in _INS:
        arr = np.ascontiguousarray(inputs[name])
        arrays[f"in_{name}"] = arr
        args.append(nc.dram_tensor(f"in_{name}", arr.shape, mybir.dt.from_np(arr.dtype), kind="ExternalInput").ap())
    out = nc.dram_tensor("out_0", (B, T, D), F32, kind="ExternalOutput").ap()
    attention_ffn_block(nc, *args, out)
    r = run_bass_kernel_spmd(nc, [arrays], core_ids=[0])
    return r.results[0]["out_0"]
```
